# Optimizing a Trainium2 kernel written in Bass

```python
import numpy as np
import jax
import jax.numpy as jnp

def _softmax(x, axis=-1):
    return jax.nn.softmax(x, axis=axis)

def _gelu(x):
    return jax.nn.gelu(x, approximate=True)

def _silu(x):
    return jax.nn.silu(x)

def _sigmoid(x):
    return jax.nn.sigmoid(x)

def _layernorm(x, axis=-1, eps=1e-05):
    m = jnp.mean(x, axis=axis, keepdims=True)
    v = jnp.var(x, axis=axis, keepdims=True)
    return (x - m) / jnp.sqrt(v + eps)

def _scatter_add(tgt, idx, src, axis=0):
    return tgt.at[idx].add(src)

def _segment_sum(src, seg, n):
    return jax.ops.segment_sum(src, seg, n)
kernel_name = 'mk_xattn_ffn_d1_seqx_r4_25c97a'

def setup_inputs(seed: int=0):
    np.random.seed(seed)
    _w = jnp.asarray

    def _rec_inputs():
        import jax
        import jax.numpy as jnp
        _rk = jax.random.key(seed)
        x = -0.0003929 + 0.9999 * jax.random.normal(jax.random.fold_in(_rk, 1), (16, 256, 512), jnp.float32)
        _lenS = 256 - jax.random.randint(jax.random.fold_in(_rk, 7), (16,), 0, max(1, 256 // 4) + 1, jnp.int32)
        _lenS2 = 256 - jax.random.randint(jax.random.fold_in(_rk, 8), (16,), 0, max(1, 256 // 4) + 1, jnp.int32)
        _ctx_2048P = jax.random.normal(jax.random.fold_in(_rk, 11), (16, 16, 512), jnp.float32)
        _ctx_2048c = jax.random.dirichlet(jax.random.fold_in(_rk, 511), 0.3 * jnp.ones((16,), jnp.float32), (16, 256))
        _ctx_2048t = jnp.einsum('bsk,bkd->bsd', _ctx_2048c, _ctx_2048P)
        _ctx_2048t = _ctx_2048t * jax.lax.rsqrt(jnp.mean(jnp.square(_ctx_2048t)) + 1e-12) * 0.953939
        ctx_2048 = 2.81802e-05 + 1.00001 * (_ctx_2048t + 0.3 * jax.random.normal(jax.random.fold_in(_rk, 611), (16, 256, 512), jnp.float32))
        return (x, ctx_2048)
    x, ctx_2048 = _rec_inputs()

    def _L0_xattn_setup():
        import jax, jax.numpy as jnp
        import numpy as np
        HIDDEN = 512
        NUM_HEADS = 16
        HEAD_DIM = HIDDEN // NUM_HEADS
        CHUNK = 256
        SCALE = HEAD_DIM ** (-0.5)

        def _chunked_causal_attention(q, k, v):
            B, H, S, D = q.shape
            n_chunks = S // CHUNK
            kc = k.reshape(B, H, n_chunks, CHUNK, D).transpose(2, 0, 1, 3, 4)
            vc = v.reshape(B, H, n_chunks, CHUNK, D).transpose(2, 0, 1, 3, 4)
            j0s = jnp.arange(n_chunks) * CHUNK
            q_idx = jnp.arange(S)[:, None]
            k_off = jnp.arange(CHUNK)[None, :]
            out0 = jnp.zeros_like(q)
            m0 = jnp.full((B, H, S, 1), -jnp.inf, dtype=q.dtype)
            s0 = jnp.zeros((B, H, S, 1), dtype=q.dtype)

            def step(carry, inputs):
                out, m, s = carry
                kj, vj, j0 = inputs
                scores = jnp.einsum('bhqd,bhkd->bhqk', q, kj) * SCALE
                causal = j0 + k_off > q_idx
                scores = jnp.where(causal[None, None], -jnp.inf, scores)
                chunk_max = scores.max(axis=-1, keepdims=True)
                new_m = jnp.maximum(m, chunk_max)
                exp_old = jnp.exp(m - new_m)
                exp_c = jnp.exp(scores - new_m)
                new_s = s * exp_old + exp_c.sum(axis=-1, keepdims=True)
                out = out * (s / new_s) * exp_old + jnp.einsum('bhqk,bhkd->bhqd', exp_c / new_s, vj)
                return ((out, new_m, new_s), None)
            (out, _, _), _ = jax.lax.scan(step, (out0, m0, s0), (kc, vc, j0s))
            return out
        key = jax.random.key(seed)
        kq, kk, kv = jax.random.split(key, 3)
        B, S = (2, 1024)
        return {'query': jax.random.normal(kq, (B, S, HIDDEN), dtype=jnp.float32), 'key': jax.random.normal(kk, (B, S, HIDDEN), dtype=jnp.float32), 'value': jax.random.normal(kv, (B, S, HIDDEN), dtype=jnp.float32)}
    _L0_xattn_all = _L0_xattn_setup()
    _L0_xattn_in = {k: v for k, v in _L0_xattn_all.items() if k in ()}
    del _L0_xattn_all

    def _L0_ffn_setup():
        import jax, jax.numpy as jnp
        import numpy as np
        EPS = 1e-05

        def fwht(x):
            orig_shape = x.shape
            n = orig_shape[-1]
            x = x.reshape(-1, n)
            h = 1
            while h < n:
                x = x.reshape(-1, n // (2 * h), 2, h)
                a, b = (x[:, :, 0, :], x[:, :, 1, :])
                x = jnp.stack([a + b, a - b], axis=2).reshape(-1, n)
                h *= 2
            return (x * (1.0 / np.sqrt(n))).reshape(orig_shape)

        def act_quant(x):
            scale = 127.0 / jnp.clip(jnp.max(jnp.abs(x), axis=-1, keepdims=True), EPS)
            q = jnp.clip(jnp.round(x * scale), -128.0, 127.0) / scale
            return x + jax.lax.stop_gradient(q - x)

        def weight_quant(w):
            scale = jnp.clip(jnp.mean(jnp.abs(w)), EPS)
            q = jnp.clip(jnp.round(w / scale), -1.0, 1.0) * scale
            return w + jax.lax.stop_gradient(q - w)

        def h_bitlinear(x, w):
            xq = act_quant(fwht(x))
            wq = weight_quant(w)
            return jnp.einsum('bsh,oh->bso', xq, wq)
        key = jax.random.key(seed)
        k1, k2, k3, k4 = jax.random.split(key, 4)
        H, I = (512, 2048)
        B, S = (2, 512)
        hidden_states = jax.random.normal(k1, (B, S, H), dtype=jnp.float32)
        w_gate = jax.random.normal(k2, (I, H), dtype=jnp.float32) * 0.02
        w_up = jax.random.normal(k3, (I, H), dtype=jnp.float32) * 0.02
        w_down = jax.random.normal(k4, (H, I), dtype=jnp.float32) * 0.02
        return {'hidden_states': hidden_states, 'w_gate': w_gate, 'w_up': w_up, 'w_down': w_down}
    _L0_ffn_all = _L0_ffn_setup()
    _L0_ffn_in = {k: v for k, v in _L0_ffn_all.items() if k in ('w_gate', 'w_up', 'w_down')}
    del _L0_ffn_all
    return {'x': x, 'ctx_2048': ctx_2048, 'L0_ffn_w_gate': _L0_ffn_in['w_gate'], 'L0_ffn_w_up': _L0_ffn_in['w_up'], 'L0_ffn_w_down': _L0_ffn_in['w_down']}

def reference(x, ctx_2048, L0_ffn_w_gate, L0_ffn_w_up, L0_ffn_w_down):
    import jax
    import jax.numpy as jnp

    def _L0_xattn_ref(query, key, value):
        import jax, jax.numpy as jnp
        import numpy as np
        HIDDEN = 512
        NUM_HEADS = 16
        HEAD_DIM = HIDDEN // NUM_HEADS
        CHUNK = 256
        SCALE = HEAD_DIM ** (-0.5)

        def _chunked_causal_attention(q, k, v):
            B, H, S, D = q.shape
            n_chunks = S // CHUNK
            kc = k.reshape(B, H, n_chunks, CHUNK, D).transpose(2, 0, 1, 3, 4)
            vc = v.reshape(B, H, n_chunks, CHUNK, D).transpose(2, 0, 1, 3, 4)
            j0s = jnp.arange(n_chunks) * CHUNK
            q_idx = jnp.arange(S)[:, None]
            k_off = jnp.arange(CHUNK)[None, :]
            out0 = jnp.zeros_like(q)
            m0 = jnp.full((B, H, S, 1), -jnp.inf, dtype=q.dtype)
            s0 = jnp.zeros((B, H, S, 1), dtype=q.dtype)

            def step(carry, inputs):
                out, m, s = carry
                kj, vj, j0 = inputs
                scores = jnp.einsum('bhqd,bhkd->bhqk', q, kj) * SCALE
                causal = j0 + k_off > q_idx
                scores = jnp.where(causal[None, None], -jnp.inf, scores)
                chunk_max = scores.max(axis=-1, keepdims=True)
                new_m = jnp.maximum(m, chunk_max)
                exp_old = jnp.exp(m - new_m)
                exp_c = jnp.exp(scores - new_m)
                new_s = s * exp_old + exp_c.sum(axis=-1, keepdims=True)
                out = out * (s / new_s) * exp_old + jnp.einsum('bhqk,bhkd->bhqd', exp_c / new_s, vj)
                return ((out, new_m, new_s), None)
            (out, _, _), _ = jax.lax.scan(step, (out0, m0, s0), (kc, vc, j0s))
            return out
        B, S, _ = query.shape
        q = query.reshape(B, S, NUM_HEADS, HEAD_DIM).transpose(0, 2, 1, 3)
        k = key.reshape(B, S, NUM_HEADS, HEAD_DIM).transpose(0, 2, 1, 3)
        v = value.reshape(B, S, NUM_HEADS, HEAD_DIM).transpose(0, 2, 1, 3)
        out = _chunked_causal_attention(q, k, v)
        return out.transpose(0, 2, 1, 3).reshape(B, S, HIDDEN)

    def _L0_ffn_ref(hidden_states, w_gate, w_up, w_down):
        import jax, jax.numpy as jnp
        import numpy as np
        EPS = 1e-05

        def fwht(x):
            orig_shape = x.shape
            n = orig_shape[-1]
            x = x.reshape(-1, n)
            h = 1
            while h < n:
                x = x.reshape(-1, n // (2 * h), 2, h)
                a, b = (x[:, :, 0, :], x[:, :, 1, :])
                x = jnp.stack([a + b, a - b], axis=2).reshape(-1, n)
                h *= 2
            return (x * (1.0 / np.sqrt(n))).reshape(orig_shape)

        def act_quant(x):
            scale = 127.0 / jnp.clip(jnp.max(jnp.abs(x), axis=-1, keepdims=True), EPS)
            q = jnp.clip(jnp.round(x * scale), -128.0, 127.0) / scale
            return x + jax.lax.stop_gradient(q - x)

        def weight_quant(w):
            scale = jnp.clip(jnp.mean(jnp.abs(w)), EPS)
            q = jnp.clip(jnp.round(w / scale), -1.0, 1.0) * scale
            return w + jax.lax.stop_gradient(q - w)

        def h_bitlinear(x, w):
            xq = act_quant(fwht(x))
            wq = weight_quant(w)
            return jnp.einsum('bsh,oh->bso', xq, wq)
        gate = h_bitlinear(hidden_states, w_gate)
        up = h_bitlinear(hidden_states, w_up)
        return h_bitlinear(jax.nn.silu(gate) * up, w_down)
    x = x + _L0_xattn_ref(_layernorm(x, axis=-1), ctx_2048, ctx_2048)
    x = x + _L0_ffn_ref(_layernorm(x, axis=-1), L0_ffn_w_gate, L0_ffn_w_up, L0_ffn_w_down)
    return x

_drawn_inputs = setup_inputs


def setup_inputs(seed=0):
    import zlib

    import numpy as np

    out = dict(_drawn_inputs(seed))
    spreads = {}
    factors = {}
    for name, (base, spread) in spreads.items():
        noise = np.random.default_rng([zlib.crc32(name.encode()), seed]).standard_normal(out[name].shape)
        drawn = base * np.exp(spread * noise) if base else spread * noise
        out[name] = jnp.asarray(drawn.astype(out[name].dtype))
    for name, factor in factors.items():
        out[name] = (out[name] * factor).astype(out[name].dtype)
    return out
```

```python
from contextlib import ExitStack

import numpy as np

import concourse.bass as bass
from concourse import mybir

F32 = mybir.dt.float32
BF16 = mybir.dt.bfloat16
ALU = mybir.AluOpType
ACT = mybir.ActivationFunctionType
AX = mybir.AxisListType

P = 128
NHEADS = 16
HD = 32
GROUPS = 4
EPS = 1e-5
ROUND = 12582912.0
MASKED = -1e38
STEPS = 12
LAG_T, LAG_V = 2, 3
TURN = (8, 9, 10, 11)
UNIT_END = (1, 3, 7, 11)
FINAL = (5, 7, 11, 15)


def exists(i, count=1 << 30):
    return not isinstance(i, int) or 0 <= i < count


def attention_ffn(nc, x, ctx, w_gate, w_up, w_down, ident_in, had_in, mask_in, out):
    B, S, D = x.shape
    FF = w_gate.shape[0]
    NC = FF // P
    KC = D // P
    TT = S // P
    NP = NC // 2
    WT = FF * D // P // D

    es = ExitStack()
    with es:
        def sb(name, shape, dt=F32):
            return es.enter_context(nc.sbuf_tensor(name, shape, dt))

        def sem(name):
            return es.enter_context(nc.semaphore(name))

        bank = [es.enter_context(nc.psum_tensor(f"bank{i}", [P, 512], F32)) for i in range(8)]

        ident = sb("ident", [P, P])
        had = sb("had", [P, P])
        ones = sb("ones", [P, P])
        maskf = sb("maskf", [P, P])
        identb = sb("identb", [P, P], BF16)
        maskb = sb("maskb", [P, 4, P], BF16)
        gate_t = sb("gate_t", [P, KC, FF], BF16)
        up_t = sb("up_t", [P, KC, FF], BF16)
        down_t = sb("down_t", [P, NC, D], BF16)
        wsum = sb("wsum", [P, 3, WT])
        wcol = sb("wcol", [P, 3])
        wscale = sb("wscale", [P, 3])
        wthr = sb("wthr", [P, 3])
        wnthr = sb("wnthr", [P, 3])
        rnd = sb("rnd", [P, 1])
        nhalf = sb("nhalf", [P, TT])
        arena = sb("arena", [P, 29 * 1024])
        wf = arena[:, 0:3 * WT * D].rearrange("p (m t n) -> p m t n", m=3, t=WT)
        tern = sb("tern", [P, WT, D], BF16)
        below = arena[:, 3 * WT * D:3 * WT * D + WT * D // 2].bitcast(BF16).rearrange("p (t n) -> p t n", t=WT)

        at = [0]

        def piece(words, pattern=None, **dims):
            a = arena[:, at[0]:at[0] + words]
            at[0] += words
            return a.rearrange(pattern, **dims) if pattern else a

        x_in = [piece(TT * D, "p (t d) -> p t d", t=TT) for _ in range(2)]
        c_in = [piece(TT * D, "p (t d) -> p t d", t=TT) for _ in range(2)]
        xn = [piece(TT * D, "p (t d) -> p t d", t=TT) for _ in range(2)]
        q_t = [piece(GROUPS * S, "p (g s) -> p g s", g=GROUPS) for _ in range(2)]
        k_z = [piece(GROUPS * 4 * S, "p (g h s) -> p g h s", g=GROUPS, h=4) for _ in range(2)]
        v_a = [piece(TT * NHEADS * (HD + 1), "p (t h e) -> p t h e", t=TT, h=NHEADS) for _ in range(2)]
        prob = [piece(512) for _ in range(3)]
        prob_t = [piece(512) for _ in range(3)]
        o_sb = [piece(TT * D, "p (t d) -> p t d", t=TT) for _ in range(2)]
        used_1 = at[0]
        at[0] = 0
        h_a = [piece(NC * S, "p (c s) -> p c s", c=NC) for _ in range(2)]
        h_b = [piece(NC * S, "p (c s) -> p c s", c=NC) for _ in range(2)]
        y_sb = [piece(FF) for _ in range(TT)]
        x1 = [piece(TT * D, "p (t d) -> p t d", t=TT) for _ in range(4)]
        r_a = piece(TT * D, "p (t c f) -> p t c f", t=TT, c=KC)
        r_b = piece(TT * D, "p (t c f) -> p t c f", t=TT, c=KC)
        z_sb = [piece(512) for _ in range(2)]
        s_sb = [piece(512) for _ in range(2)]
        bro = [piece(2 * S) for _ in range(2)]
        assert max(at[0], used_1) <= 29 * 1024, (at[0], used_1)
        rot_t = sb("rot_t", [P, KC, P])
        qm = sb("qm", [P, D])
        q_i = sb("q_i", [P, D], BF16)
        xq_t = [sb(f"xq_t{n}", [P, KC, S], BF16) for n in range(2)]
        q2_i = tern[:, 0:TT * 4, :].rearrange("p (t c) n -> p t (c n)", t=TT)
        q2_t = tern[:, TT * 4:2 * TT * 4, :].rearrange("p (t c) n -> p t (c n)", t=TT).rearrange(
            "p t (c n) -> p t c n", n=P)
        y_out = [sb(f"y_out{n}", [P, D]) for n in range(TT)]
        diag = sb("diag", [P, TT, P])
        bn = sb("bn", [P, TT, 6])
        mv = sb("mv", [P, TT, 2])
        vareps = sb("vareps", [P, TT])
        rstd = sb("rstd", [P, TT])
        rstd_s = sb("rstd_s", [P, TT])
        nmax = sb("nmax", [P, STEPS, 4])
        rinv = sb("rinv", [P, 4, 8])
        amax = sb("amax", [P, TT])
        m1 = sb("m1", [P, TT])
        r1 = sb("r1", [P, TT])
        qs1 = sb("qs1", [P, TT])
        cg = sb("cg", [P, TT])
        ku = [sb(f"ku{n}", [P, TT]) for n in range(4)]
        amax2 = sb("amax2", [P, TT])
        m2 = sb("m2", [P, TT])
        r2 = sb("r2", [P, TT])
        qs2 = sb("qs2", [P, TT])
        dd = [sb(f"dd{n}", [P, TT]) for n in range(2)]

        const_in = sem("const_in")
        const_ok = sem("const_ok")
        w_in = [sem(f"w_in{m}") for m in range(3)]
        w_summed = sem("w_summed")
        w_total = sem("w_total")
        w_chain = sem("w_chain")
        w_below = sem("w_below")
        w_tern = sem("w_tern")
        w_turned = sem("w_turned")
        w_out_d = sem("w_out_d")
        w_out_a = sem("w_out_a")
        x_loaded = [sem(f"x_loaded{n}") for n in range(2)]
        c_loaded = [sem(f"c_loaded{n}") for n in range(2)]
        zeroed = sem("zeroed")
        ln_chain = sem("ln_chain")
        var_ready = sem("var_ready")
        rstd_ready = sem("rstd_ready")
        xn_ready = sem("xn_ready")
        v_ready = sem("v_ready")
        turned = sem("turned")
        turned_a = sem("turned_a")
        turned_d = sem("turned_d")
        scored = sem("scored")
        max_ready = sem("max_ready")
        exp_done = sem("exp_done")
        p_turned = sem("p_turned")
        pt_act = sem("pt_act")
        pt_dve = sem("pt_dve")
        pv_done = sem("pv_done")
        rinv_ready = sem("rinv_ready")
        o_ready = sem("o_ready")
        x1_ready = sem("x1_ready")
        x1_stored = [sem(f"x1_stored{n}") for n in range(2)]
        f_loaded = [sem(f"f_loaded{n}") for n in range(2)]
        f_ln = sem("f_ln")
        f_var = sem("f_var")
        f_rstd = sem("f_rstd")
        f_xn = sem("f_xn")
        f_rot = sem("f_rot")
        f_rot_t = sem("f_rot_t")
        f_rot_e = sem("f_rot_e")
        f_had = sem("f_had")
        f_stat = sem("f_stat")
        f_qs = sem("f_qs")
        f_qm = sem("f_qm")
        f_qi = sem("f_qi")
        f_qt = sem("f_qt")
        f_xq = sem("f_xq")
        f_diag = sem("f_diag")
        f_brop = sem("f_brop")
        f_bro = sem("f_bro")
        gu_done = sem("gu_done")
        z_ready = sem("z_ready")
        s_ready = sem("s_ready")
        h_ready = sem("h_ready")
        b1_done = sem("b1_done")
        b2_done = sem("b2_done")
        b3_done = sem("b3_done")
        b4_done = sem("b4_done")
        y_done = sem("y_done")
        y_out_sem = sem("y_evac")
        y_stat = sem("y_stat")
        y_qs = sem("y_qs")
        dd_ready = sem("dd_ready")
        y_qm = sem("y_qm")
        y_qi = sem("y_qi")
        q2_turned = sem("q2_turned")
        q2_ready = sem("q2_ready")
        d_done = sem("d_done")
        o2_ready = sem("o2_ready")
        stored = [sem(f"stored{n}") for n in range(TT)]

        block = es.enter_context(nc.Block())

        weights = (w_gate, w_up, w_down)
        weights_t = (gate_t, up_t, down_t)

        def w_blocks(m, t):
            if m < 2:
                return weights_t[m][:, :, t * P:(t + 1) * P]
            a, b = t // (FF // D), t % (FF // D)
            return down_t[:, b * KC:(b + 1) * KC, a * P:(a + 1) * P]

        S_BANK, T_BANK, O_BANK, X_BANK = (0, 1, 2), (3, 4), (5, 6), 7

        def step_of(s):
            if s < GROUPS:
                return 0, s, 0, 4, P
            return 1, (s - GROUPS) // 2, 2 * ((s - GROUPS) % 2), 2, S

        def unit_of(s):
            t, g, _, _, _ = step_of(s)
            return 2 * t + g // 2

        def batches(engine, body, count):
            body(0)
            body(1)
            with engine.Fori(1, count // 2 - 1) as j:
                body(j * 2)
                body(j * 2 + 1, 1)
            body(count - 2)
            body(count - 1)

        def par(i, odd):
            return i % 2 if isinstance(i, int) else odd

        @block.sync
        def _(sp):
            for dst, src in ((ident, ident_in), (had, had_in), (maskf, mask_in)):
                sp.dma_start(dst[:, :], src).then_inc(const_in, 16)
            for m in range(2):
                sp.dma_start(wf[:, m, :, :], weights[m].rearrange("(t p) n -> p t n", p=P)).then_inc(w_in[m], 16)
            for a in range(D // P):
                sp.dma_start(wf[:, 2, a * KC:(a + 1) * KC, :].rearrange("p b n -> p (b n)"),
                             w_down[a * P:(a + 1) * P, :]).then_inc(w_in[2], 16)

            def load(b, p):
                sp.dma_start(x_in[p], x[b:b + 1].rearrange("o (t p) d -> p (o t) d", p=P)
                             if isinstance(b, int) else
                             x[bass.ds(b, 1)].rearrange("o (t p) d -> p (o t) d", p=P)
                             ).then_inc(x_loaded[p], 16)
                sp.dma_start(c_in[p], ctx[b:b + 1].rearrange("o (t p) d -> p (o t) d", p=P)
                             if isinstance(b, int) else
                             ctx[bass.ds(b, 1)].rearrange("o (t p) d -> p (o t) d", p=P)
                             ).then_inc(c_loaded[p], 16)

            sp.wait_ge(w_tern, 3)
            load(0, 0)
            load(1, 1)

            def store_1(b, odd=0):
                p = par(b, odd)
                sp.wait_ge(x1_ready, b * TT + TT)
                dst = out[b:b + 1] if isinstance(b, int) else out[bass.ds(b, 1)]
                sp.dma_start(dst.rearrange("o (t p) d -> p (o t) d", p=P), o_sb[p]).then_inc(x1_stored[p], 16)
                if not (isinstance(b, int) and b + 2 >= B):
                    sp.wait_ge(v_ready, b + 1)
                    sp.wait_ge(turned, b * 4 + 4)
                    load(b + 2, p)

            batches(sp, store_1, B)

            def load_2(i, odd, q):
                src = out[i:i + 1] if isinstance(i, int) else out[bass.ds(i, 1)]
                sp.dma_start(x1[q], src.rearrange("o (t p) d -> p (o t) d", p=P)).then_inc(f_loaded[odd], 16)

            for p in range(2):
                sp.wait_ge(x1_stored[p], 16 * (B // 2))
            load_2(0, 0, 0)
            load_2(1, 1, 1)

            def store_2(i, odd=0):
                for t in range(TT):
                    sp.wait_ge(o2_ready, i * TT + t + 1)
                    rows = (out[i:i + 1] if isinstance(i, int) else out[bass.ds(i, 1)])
                    sp.dma_start(rows[:, t * P:(t + 1) * P, :].rearrange("o p d -> p (o d)"),
                                 y_out[t][:, :]).then_inc(stored[t], 16)

            def quad(i, q):
                if exists(i - 2):
                    store_2(i - 2, q % 2)
                if not (isinstance(i, int) and i + 2 >= B):
                    sp.wait_ge(f_xn, i * 2 + 2)
                    load_2(i + 2, q % 2, (q + 2) % 4)

            for i in range(4):
                quad(i, i)
            with sp.Fori(1, B // 4 - 1) as j:
                for q in range(4):
                    quad(j * 4 + q, q)
            for i in range(B - 4, B):
                quad(i, i % 4)
            for i in range(B, B + 2):
                store_2(i - 2)
            for t in range(TT):
                sp.wait_ge(stored[t], 16 * B)

        @block.gpsimd
        def _(pool):
            pool.memset(ones[:, :], 1.0).then_inc(const_ok, 1)
            pool.memset(rnd[:, :], ROUND).then_inc(const_ok, 1)
            pool.memset(nhalf[:, :], -0.5).then_inc(const_ok, 1)
            pool.wait_ge(w_tern, 3)
            for p in range(2):
                pool.memset(k_z[p], 0.0).then_inc(zeroed, 1)
                pool.memset(v_a[p], 1.0).then_inc(zeroed, 1)
            pool.wait_ge(zeroed, 4)

            def prepare(b, p):
                pool.wait_ge(c_loaded[p], (b // 2) * 16 + 16 if isinstance(b, int) else (b - p) * 8 + 16)
                if exists(b - 2):
                    pool.wait_ge(pv_done, b * STEPS - STEPS)
                pool.wait_ge(var_ready, b + 1)
                pool.tensor_tensor(rstd[:, :], vareps[:, :], nhalf[:, :], ALU.pow).then_inc(rstd_ready, 1)
                pool.tensor_copy(v_a[p][:, :, :, 0:HD],
                                 c_in[p].rearrange("p t (h e) -> p t h e", e=HD)).then_inc(v_ready, 1)

            def residual(b, p, t):
                pool.wait_ge(o_ready, b * 4 + 2 * t + 2)
                pool.tensor_tensor(o_sb[p][:, t, :], o_sb[p][:, t, :], x_in[p][:, t, :],
                                   ALU.add).then_inc(x1_ready, 1)

            prepare(0, 0)

            def body(b, odd=0):
                p = par(b, odd)
                if exists(b - 1):
                    residual(b - 1, 1 - p, 1)
                if not (isinstance(b, int) and b + 1 >= B):
                    prepare(b + 1, 1 - p)
                residual(b, p, 0)

            batches(pool, body, B)
            residual(B - 1, 1, 1)

            def rotate(i, p):
                pool.wait_ge(f_var, i + 1)
                pool.tensor_tensor(rstd[:, :], vareps[:, :], nhalf[:, :], ALU.pow).then_inc(f_rstd, 1)
                pool.wait_ge(f_xn, i * 2 + 2)
                a = r_a.rearrange("p t (u v) f -> p t u v f", v=2)
                b_ = r_b.rearrange("p t (u v) f -> p t u v f", v=2)
                for t in range(TT):
                    pool.tensor_tensor(b_[:, t, :, 0, :], a[:, t, :, 0, :], a[:, t, :, 1, :], ALU.add).then_inc(f_rot, 1)
                    pool.tensor_tensor(b_[:, t, :, 1, :], a[:, t, :, 0, :], a[:, t, :, 1, :], ALU.subtract).then_inc(f_rot, 1)
                pool.wait_ge(f_rot, i * 8 + 4)
                for t in range(TT):
                    pool.tensor_tensor(r_a[:, t, 0:2, :], r_b[:, t, 0:2, :], r_b[:, t, 2:4, :], ALU.add).then_inc(f_rot, 1)
                    pool.tensor_tensor(r_a[:, t, 2:4, :], r_b[:, t, 0:2, :], r_b[:, t, 2:4, :], ALU.subtract).then_inc(f_rot, 1)

            def stages(i, p, which):
                a, b_ = h_a[p], h_b[p]
                for g in which:
                    lo = 4 * g
                    pool.wait_ge(b1_done, i * 8 + 2 * g + 2)
                    pool.tensor_tensor(a[:, lo:lo + 2, :], b_[:, lo:lo + 2, :], b_[:, lo + 2:lo + 4, :], ALU.add).then_inc(b2_done, 1)
                    pool.tensor_tensor(a[:, lo + 2:lo + 4, :], b_[:, lo:lo + 2, :], b_[:, lo + 2:lo + 4, :], ALU.subtract).then_inc(b2_done, 1)
                    if g % 2 == 1:
                        lo -= 4
                        pool.wait_ge(b2_done, i * 8 + 2 * g + 2)
                        pool.tensor_tensor(b_[:, lo:lo + 4, :], a[:, lo:lo + 4, :], a[:, lo + 4:lo + 8, :], ALU.add).then_inc(b3_done, 1)
                        pool.tensor_tensor(b_[:, lo + 4:lo + 8, :], a[:, lo:lo + 4, :], a[:, lo + 4:lo + 8, :], ALU.subtract).then_inc(b3_done, 1)
                    if g == 3:
                        pool.wait_ge(b3_done, i * 4 + 4)
                        for t in range(TT):
                            c = slice(t * P, (t + 1) * P)
                            pool.tensor_tensor(a[:, 0:8, c], b_[:, 0:8, c], b_[:, 8:16, c], ALU.add).then_inc(b4_done, 1)
                            pool.tensor_tensor(a[:, 8:16, c], b_[:, 0:8, c], b_[:, 8:16, c], ALU.subtract).then_inc(b4_done, 1)

            rotate(0, 0)
            rotate(1, 1)

            def body2(i, odd=0):
                p = par(i, odd)
                if exists(i - 1):
                    stages(i - 1, 1 - p, (3,))
                if exists(i, B):
                    stages(i, p, (0, 1, 2))
                if exists(i + 2, B):
                    rotate(i + 2, p)

            batches(pool, body2, B)
            body2(B)

        @block.scalar
        def _(act):
            for n in range(3 * WT // 2):
                if n % 2 == 1:
                    m, t = divmod(2 * n, WT)
                    act.wait_ge(w_turned, n + 1)
                    for k in range(2):
                        ins = act.activation(
                            w_blocks(m, t + k),
                            bank[n % 4][:, :].bitcast(BF16).rearrange("p (k c f) -> p k c f", k=2, c=KC)[:, k],
                            ACT.Copy)
                    ins.then_inc(w_out_a, 1)

            def softmax(b, p, s):
                _, _, _, heads, keys = step_of(s)
                n = b * STEPS + s
                act.wait_ge(max_ready, n + 1)
                if not (isinstance(b, int) and b * STEPS + s < 3):
                    act.wait_ge(p_turned, n - 2)
                for h in range(heads):
                    ins = act.activation(prob[s % 3][:, h * keys:(h + 1) * keys],
                                         bank[S_BANK[s % 3]][:, h * keys:(h + 1) * keys],
                                         ACT.Exp, bias=nmax[:, s, h:h + 1])
                ins.then_inc(exp_done, 1)

            def out_pt(b, s):
                n = b * STEPS + s
                act.wait_ge(p_turned, n + 1)
                if not (isinstance(b, int) and b * STEPS + s < 3):
                    act.wait_ge(pv_done, n - 2)
                act.activation(prob_t[s % 3], bank[T_BANK[s % 2]][:, :], ACT.Copy).then_inc(pt_act, 1)

            def out_turn(b, p, k):
                t = k // 2
                act.wait_ge(turned, b * 4 + k + 1)
                src = bank[X_BANK][:, :].rearrange("p (g s) -> p g s", g=GROUPS)
                if k % 2 == 0:
                    act.activation(q_t[p][:, :, t * P:(t + 1) * P], src, ACT.Copy).then_inc(turned_a, 1)
                else:
                    for h in range(2):
                        r = slice(h * HD, (h + 1) * HD)
                        ins = act.activation(k_z[p][r, :, h, t * P:(t + 1) * P], src[r], ACT.Copy)
                    ins.then_inc(turned_a, 1)

            act.wait_ge(zeroed, 4)
            for k in range(4):
                out_turn(0, 0, k)

            def body(b, odd=0):
                p = par(b, odd)
                more = not (isinstance(b, int) and b + 1 >= B)
                for s in range(STEPS):
                    if s == 0 and exists(b - 1):
                        out_turn(b, p, 3)
                    softmax(b, p, s)
                    if s % 2 == 0 and (s >= 2 or exists(b - 1)):
                        out_pt(b if s >= 2 else b - 1, (s - 2) % STEPS)
                    if more:
                        for k in range(3):
                            if s == TURN[k] + 1:
                                out_turn(b + 1, 1 - p, k)

            batches(act, body, B)
            out_pt(B - 1, STEPS - 2)

            def prep_turn(i, t):
                act.wait_ge(f_rot_t, i * 2 + t + 1)
                act.activation(rot_t[:, :, :], bank[7][:, :].rearrange("p (c f) -> p c f", c=KC),
                               ACT.Copy).then_inc(f_rot_e, 1)

            def prep_round(i, t):
                act.wait_ge(f_qs, i * 2 + t + 1)
                act.activation(qm[:, :], bank[7][:, :], ACT.Identity, scale=qs1[:, t:t + 1],
                               bias=rnd[:, 0:1]).then_inc(f_qm, 1)

            def prep_xq(i, p, t):
                act.wait_ge(f_qt, i * 2 + t + 1)
                act.activation(xq_t[p][:, :, t * P:(t + 1) * P],
                               bank[7][:, 0:D // 2].bitcast(BF16).rearrange("p (c f) -> p c f", c=KC),
                               ACT.Copy).then_inc(f_xq, 1)

            def prep_bro(i, p):
                act.wait_ge(f_brop, i + 1)
                act.activation(bro[p], bank[7][:, :], ACT.Copy).then_inc(f_bro, 1)

            def silu(i, c):
                act.wait_ge(z_ready, i * NP + c + 1)
                act.activation(s_sb[c % 2], z_sb[c % 2], ACT.Silu).then_inc(s_ready, 1)

            def out_y(i, t, q):
                act.wait_ge(y_done, i * 8 + 4 * t + q + 1)
                act.activation(y_sb[t][:, q * 512:(q + 1) * 512], bank[4 + q % 2][:, :],
                               ACT.Copy).then_inc(y_out_sem, 1)

            def round_y(i, t):
                act.wait_ge(y_qs, i * 2 + t + 1)
                act.activation(y_sb[t], y_sb[t], ACT.Identity, scale=qs2[:, t:t + 1],
                               bias=rnd[:, 0:1]).then_inc(y_qm, 1)

            def out_q2(i, t, k):
                act.wait_ge(q2_turned, i * 4 + 2 * t + k + 1)
                act.activation(q2_t[:, t, 8 * k:8 * k + 8, :],
                               bank[4 + k][:, :].bitcast(BF16).rearrange("p (c f) -> p c f", c=8),
                               ACT.Copy).then_inc(q2_ready, 1)

            for t in range(TT):
                prep_turn(0, t)
                prep_round(0, t)
                if t == 1:
                    prep_bro(0, 0)
                prep_xq(0, 0, t)

            def body2(i, odd=0):
                p = par(i, odd)
                here, before, two, ahead = exists(i, B), exists(i - 1, B), exists(i - 2, B), exists(i + 1, B)
                for c in range(NP):
                    if here:
                        silu(i, c)
                    if c == 0 and two:
                        out_q2(i - 2, 0, 0)
                        out_q2(i - 2, 0, 1)
                    if c == 0 and ahead:
                        prep_turn(i + 1, 0)
                    if c == 1 and two:
                        round_y(i - 2, 1)
                    if c == 1 and ahead:
                        prep_round(i + 1, 0)
                    if c == 2 and two:
                        out_q2(i - 2, 1, 0)
                        out_q2(i - 2, 1, 1)
                    if c == 2 and ahead:
                        prep_xq(i + 1, 1 - p, 0)
                    if c == 3 and ahead:
                        prep_turn(i + 1, 1)
                    if c == 4 and ahead:
                        prep_round(i + 1, 1)
                    if c == 7 and before:
                        round_y(i - 1, 0)
                    if c >= 4 and before:
                        for q in (2 * (c - 4), 2 * (c - 4) + 1):
                            out_y(i - 1, q // 4, q % 4)
                    if c == 5 and ahead:
                        prep_bro(i + 1, 1 - p)
                    if c == 6 and ahead:
                        prep_xq(i + 1, 1 - p, 1)

            batches(act, body2, B)
            body2(B)
            body2(B + 1)

        @block.vector
        def _(dve):
            dve.wait_ge(const_in, 48)
            dve.tensor_copy(identb[:, :], ident[:, :]).then_inc(const_ok, 1)
            for h in range(4):
                ins = dve.tensor_copy(maskb[:, h, :], maskf[:, :])
            ins.then_inc(const_ok, 1)
            chain = 0
            for m in range(3):
                dve.wait_ge(w_in[m], 64 if m == 2 else 16)
                dve.tensor_reduce(wsum[:, m, :], wf[:, m, :, :], AX.X, ALU.add,
                                  apply_absolute_value=True).then_inc(w_chain, 1)
                chain += 1
                dve.wait_ge(w_chain, chain)
                dve.tensor_reduce(wcol[:, m:m + 1], wsum[:, m, :], AX.X, ALU.add).then_inc(w_summed, 1)
                dve.wait_ge(w_total, m + 1)
                dve.tensor_scalar(wscale[:, m:m + 1], bank[4][:, m:m + 1], 1.0 / (FF * D), EPS,
                                  ALU.mult, ALU.max).then_inc(w_chain, 1)
                chain += 1
                dve.wait_ge(w_chain, chain)
                dve.tensor_scalar(wthr[:, m:m + 1], wscale[:, m:m + 1], 0.5, None, ALU.mult).then_inc(w_chain, 1)
                dve.tensor_scalar(wnthr[:, m:m + 1], wscale[:, m:m + 1], -0.5, None, ALU.mult).then_inc(w_chain, 1)
                chain += 2
                dve.wait_ge(w_chain, chain)
                dve.tensor_scalar(below, wf[:, m, :, :], wnthr[:, m:m + 1], None, ALU.is_lt).then_inc(w_chain, 1)
                chain += 1
                dve.wait_ge(w_chain, chain)
                if m:
                    dve.wait_ge(w_turned, m * WT // 2)
                dve.scalar_tensor_tensor(out=tern[:, :, :], in0=wf[:, m, :, :], scalar=wthr[:, m:m + 1],
                                         in1=below, op0=ALU.is_gt, op1=ALU.subtract).then_inc(w_tern, 1)
                for n in range(m * WT // 2, (m + 1) * WT // 2):
                    if n % 2 == 0:
                        t = 2 * n - m * WT
                        dve.wait_ge(w_turned, n + 1)
                        for k in range(2):
                            ins = dve.tensor_copy(
                                w_blocks(m, t + k),
                                bank[n % 4][:, :].bitcast(BF16).rearrange("p (k c f) -> p k c f", k=2, c=KC)[:, k])
                        ins.then_inc(w_out_d, 1)

            def moments(b, src, chain_sem, per):
                for t in range(TT):
                    dve.bn_stats(bn[:, t, :], src[:, t, :]).then_inc(chain_sem, 1)
                dve.wait_ge(chain_sem, b * per + 2)
                dve.memset(vareps[:, :], 0.0).then_inc(chain_sem, 1)
                for t in range(TT):
                    dve.bn_aggr(mv[:, t, :], bn[:, t, :]).then_inc(chain_sem, 1)
                dve.wait_ge(chain_sem, b * per + 5)

            def norm_1(b, p):
                dve.wait_ge(x_loaded[p], (b // 2) * 16 + 16 if isinstance(b, int) else (b - p) * 8 + 16)
                moments(b, x_in[p], ln_chain, 6)
                dve.tensor_scalar(vareps[:, :], mv[:, :, 1], EPS, None, ALU.add).then_inc(var_ready, 1)

            def norm_2(b, p):
                dve.wait_ge(rstd_ready, b + 1)
                dve.tensor_scalar(rstd_s[:, :], rstd[:, :], float(HD) ** -0.5, None, ALU.mult).then_inc(ln_chain, 1)
                dve.wait_ge(ln_chain, b * 6 + 6)
                for t in range(TT):
                    dve.tensor_scalar(xn[p][:, t, :], x_in[p][:, t, :], mv[:, t, 0:1], rstd_s[:, t:t + 1],
                                      ALU.subtract, ALU.mult).then_inc(xn_ready, 1)

            def out_turn(b, p, k):
                t = k // 2
                dve.wait_ge(turned, b * 4 + k + 1)
                src = bank[X_BANK][:, :].rearrange("p (g s) -> p g s", g=GROUPS)
                for h in range(2, 4):
                    r = slice(h * HD, (h + 1) * HD)
                    ins = dve.tensor_copy(k_z[p][r, :, h, t * P:(t + 1) * P], src[r])
                ins.then_inc(turned_d, 1)

            def row_max(b, s):
                _, _, _, heads, keys = step_of(s)
                dve.wait_ge(scored, b * STEPS + s + 1)
                dve.tensor_reduce(nmax[:, s, 0:heads],
                                  bank[S_BANK[s % 3]][:, :].rearrange("p (h k) -> p h k", h=heads),
                                  AX.X, ALU.max, negate=True).then_inc(max_ready, 1)

            def out_pt(b, s):
                n = b * STEPS + s
                dve.wait_ge(p_turned, n + 1)
                if not (isinstance(b, int) and b * STEPS + s < 3):
                    dve.wait_ge(pv_done, n - 2)
                dve.tensor_copy(prob_t[s % 3], bank[T_BANK[s % 2]][:, :]).then_inc(pt_dve, 1)

            def final(b, p, u):
                t, half = divmod(u, 2)
                dve.wait_ge(pv_done, b * STEPS + UNIT_END[u] + 1)
                o = bank[O_BANK[u % 2]][:, 0:8 * (HD + 1)].rearrange("p (h e) -> p h e", h=8)
                dve.reciprocal(rinv[:, u, :], o[:, :, HD]).then_inc(rinv_ready, 1)
                dve.wait_ge(rinv_ready, b * 4 + u + 1)
                if exists(b - 2) and u == 0:
                    dve.wait_ge(x1_stored[p], (b // 2) * 16 if isinstance(b, int) else (b - p) * 8)
                dve.tensor_tensor(o_sb[p][:, t, half * 256:(half + 1) * 256].rearrange("p (h e) -> p h e", h=8),
                                  o[:, :, 0:HD], rinv[:, u, :].unsqueeze(2).to_broadcast([P, 8, HD]),
                                  ALU.mult).then_inc(o_ready, 1)

            dve.wait_ge(zeroed, 4)
            norm_1(0, 0)
            norm_2(0, 0)
            out_turn(0, 0, 1)
            out_turn(0, 0, 3)

            def body(b, odd=0):
                p = par(b, odd)
                more = not (isinstance(b, int) and b + 1 >= B)
                for s in range(STEPS):
                    if s == 0 and exists(b - 1):
                        out_turn(b, p, 3)
                    row_max(b, s)
                    if s % 2 == 1 and (s >= 2 or exists(b - 1)):
                        out_pt(b if s >= 2 else b - 1, (s - 2) % STEPS)
                    for u in range(3):
                        if s == FINAL[u]:
                            final(b, p, u)
                    if s == FINAL[3] - STEPS and exists(b - 1):
                        final(b - 1, 1 - p, 3)
                    if more:
                        if s == 6:
                            norm_1(b + 1, 1 - p)
                        if s == 7:
                            norm_2(b + 1, 1 - p)
                        if s == TURN[1] + 1:
                            out_turn(b + 1, 1 - p, 1)

            batches(dve, body, B)
            out_pt(B - 1, STEPS - 1)
            final(B - 1, 1, 3)

            def f_norm(i, p, q):
                dve.wait_ge(f_loaded[p], (i // 2) * 16 + 16 if isinstance(i, int) else (i - p) * 8 + 16)
                moments(i, x1[q], f_ln, 5)
                dve.tensor_scalar(vareps[:, :], mv[:, :, 1], EPS, None, ALU.add).then_inc(f_var, 1)
                dve.wait_ge(f_rstd, i + 1)
                if exists(i - 1):
                    dve.wait_ge(f_rot_t, i * 2)
                for t in range(TT):
                    dve.tensor_scalar(r_a[:, t, :, :].rearrange("p c f -> p (c f)"), x1[q][:, t, :],
                                      mv[:, t, 0:1], rstd[:, t:t + 1],
                                      ALU.subtract, ALU.mult).then_inc(f_xn, 1)

            def f_scale(i, q, t):
                root = float(D) ** -0.5
                dve.wait_ge(f_had, i * 2 + t + 1)
                c = slice(t, t + 1)
                k = i * 10 + t * 5
                dve.tensor_reduce(amax[:, c], bank[7][:, :], AX.X, ALU.max,
                                  apply_absolute_value=True).then_inc(f_stat, 1)
                dve.wait_ge(f_stat, k + 1)
                dve.tensor_scalar(m1[:, c], amax[:, c], root, EPS, ALU.mult, ALU.max).then_inc(f_stat, 1)
                dve.wait_ge(f_stat, k + 2)
                dve.reciprocal(r1[:, c], m1[:, c]).then_inc(f_stat, 1)
                dve.wait_ge(f_stat, k + 3)
                dve.tensor_scalar(qs1[:, c], r1[:, c], 127.0 * root, None, ALU.mult).then_inc(f_qs, 1)
                dve.tensor_scalar(cg[:, c], m1[:, c], wscale[:, 0:1], 1.0 / 127, ALU.mult, ALU.mult).then_inc(f_stat, 1)
                dve.tensor_scalar(ku[q][:, c], m1[:, c], wscale[:, 1:2], float(FF) ** -0.5 / 127,
                                  ALU.mult, ALU.mult).then_inc(f_stat, 1)
                dve.wait_ge(f_stat, k + 5)
                dve.tensor_scalar(diag[:, t, :], ident[:, :], cg[:, c], None, ALU.mult).then_inc(f_diag, 1)

            def f_int(i, t):
                dve.wait_ge(f_qm, i * 2 + t + 1)
                dve.tensor_scalar(q_i[:, :], qm[:, :], -ROUND, 127.0, ALU.add, ALU.min).then_inc(f_qi, 1)

            def gate_scale(i, p, c):
                dve.wait_ge(gu_done, i * NP + c + 1)
                if c == 0:
                    dve.wait_ge(f_bro, i + 1)
                dve.tensor_tensor(z_sb[c % 2], bank[2 * (c % 2)][:, :], bro[p], ALU.mult).then_inc(z_ready, 1)

            def times_up(i, p, c):
                dve.wait_ge(s_ready, i * NP + c + 1)
                if c == 0 and exists(i - 2):
                    dve.wait_ge(y_done, i * 8 - 8)
                dve.tensor_tensor(h_a[p][:, 2 * c:2 * c + 2, :].rearrange("p c s -> p (c s)"),
                                  s_sb[c % 2], bank[2 * (c % 2) + 1][:, :], ALU.mult).then_inc(h_ready, 1)

            def stage_1(i, p, g):
                a = h_a[p][:, 4 * g:4 * g + 4, :].rearrange("p (u v) s -> p u v s", v=2)
                b_ = h_b[p][:, 4 * g:4 * g + 4, :].rearrange("p (u v) s -> p u v s", v=2)
                dve.wait_ge(h_ready, i * NP + 2 * g + 2)
                if g == 0 and exists(i - 2):
                    dve.wait_ge(b4_done, i * 4 - 4)
                dve.tensor_tensor(b_[:, :, 0, :], a[:, :, 0, :], a[:, :, 1, :], ALU.add).then_inc(b1_done, 1)
                dve.tensor_tensor(b_[:, :, 1, :], a[:, :, 0, :], a[:, :, 1, :], ALU.subtract).then_inc(b1_done, 1)

            def y_scale(i, q, t):
                p = q % 2
                c = slice(t, t + 1)
                k = i * 6 + t * 3
                dve.wait_ge(y_out_sem, i * 8 + 4 * t + 4)
                dve.tensor_reduce(amax2[:, c], y_sb[t], AX.X, ALU.max, apply_absolute_value=True).then_inc(y_stat, 1)
                dve.wait_ge(y_stat, k + 1)
                dve.tensor_scalar(m2[:, c], amax2[:, c], ku[q][:, c], EPS, ALU.mult, ALU.max).then_inc(y_stat, 1)
                dve.wait_ge(y_stat, k + 2)
                dve.reciprocal(r2[:, c], m2[:, c]).then_inc(y_stat, 1)
                dve.wait_ge(y_stat, k + 3)
                dve.tensor_scalar(qs2[:, c], r2[:, c], ku[q][:, c], 127.0, ALU.mult, ALU.mult).then_inc(y_qs, 1)
                dve.tensor_scalar(dd[p][:, c], m2[:, c], wscale[:, 2:3], 1.0 / 127, ALU.mult, ALU.mult).then_inc(dd_ready, 1)

            def y_int(i, t):
                dve.wait_ge(y_qm, i * 2 + t + 1)
                if exists(i - 1):
                    dve.wait_ge(q2_turned, i * 4 - 2 + 2 * t)
                dve.tensor_scalar(q2_i[:, t, :], y_sb[t], -ROUND, 127.0, ALU.add, ALU.min).then_inc(y_qi, 1)

            def finish(i, p, q, t):
                dve.wait_ge(d_done, i * 2 + t + 1)
                if exists(i - 1):
                    dve.wait_ge(stored[t], i * 16)
                if t == 0:
                    dve.wait_ge(dd_ready, i * 2 + 2)
                dve.scalar_tensor_tensor(out=y_out[t][:, :], in0=bank[6][:, :], scalar=dd[p][:, t:t + 1],
                                         in1=x1[q][:, t, :], op0=ALU.mult, op1=ALU.add).then_inc(o2_ready, 1)

            f_norm(0, 0, 0)
            for t in range(TT):
                f_scale(0, 0, t)
                f_int(0, t)
            f_norm(1, 1, 1)

            def body2(i, q):
                p = q % 2
                here, before, two, ahead = exists(i, B), exists(i - 1, B), exists(i - 2, B), exists(i + 1, B)
                for c in range(NP):
                    if here:
                        gate_scale(i, p, c)
                    if c == 0 and two:
                        y_scale(i - 2, (q + 2) % 4, 1)
                    if c == 1 and two:
                        y_int(i - 2, 1)
                    if c == 2 and ahead:
                        f_int(i + 1, 0)
                    if c == 2 and two:
                        finish(i - 2, p, (q + 2) % 4, 0)
                    if c == 4 and two:
                        finish(i - 2, p, (q + 2) % 4, 1)
                    if c == 4 and ahead:
                        f_scale(i + 1, (q + 1) % 4, 1)
                    if c == 5 and ahead:
                        f_int(i + 1, 1)
                    if c == 6 and before:
                        y_scale(i - 1, (q + 3) % 4, 0)
                    if c == 7 and before:
                        y_int(i - 1, 0)
                    if here:
                        times_up(i, p, c)
                        if c % 2 == 1:
                            stage_1(i, p, c // 2)
                    if c == 1 and ahead:
                        f_scale(i + 1, (q + 1) % 4, 0)
                    if c == 6 and exists(i + 2, B):
                        f_norm(i + 2, p, (q + 2) % 4)

            for i in range(4):
                body2(i, i)
            with dve.Fori(1, B // 4 - 1) as j:
                for q in range(4):
                    body2(j * 4 + q, q)
            for i in range(B - 4, B + 2):
                body2(i, i % 4)

        @block.tensor
        def _(pe):
            pe.wait_ge(const_ok, 5)
            for m in range(3):
                pe.wait_ge(w_summed, m + 1)
                pe.matmul(bank[4][:, m:m + 1], ones[:, :], wcol[:, m:m + 1], start=True, stop=True).then_inc(w_total, 1)
                pe.wait_ge(w_tern, m + 1)
                for n in range(m * WT // 2, (m + 1) * WT // 2):
                    if n >= 4:
                        pe.wait_ge(w_out_a if n % 2 else w_out_d, (n - 4) // 2 + 1)
                    for k in range(8):
                        t = 2 * n - m * WT + k // 4
                        ins = pe.transpose(bank[n % 4][:, 64 * k:64 * k + 64].bitcast(BF16),
                                           tern[:, t, (k % 4) * P:(k % 4 + 1) * P], identb[:, :])
                    ins.then_inc(w_turned, 1)
            pe.wait_ge(w_out_a, 3 * WT // 4)
            pe.wait_ge(w_out_d, 3 * WT // 4)
            pe.wait_ge(w_turned, 3 * WT // 2)

            def turn(b, p, k):
                t = k // 2
                if k == 0:
                    pe.wait_ge(xn_ready, b * 2 + 2)
                    pe.wait_ge(c_loaded[p], (b // 2) * 16 + 16 if isinstance(b, int) else (b - p) * 8 + 16)
                if not (isinstance(b, int) and b == 0 and k == 0):
                    pe.wait_ge(turned_a, b * 4 + k)
                    if k % 2 == 0:
                        pe.wait_ge(turned_d, b * 2 + k // 2)
                src = (c_in if k % 2 else xn)[p]
                for g in range(GROUPS):
                    ins = pe.transpose(bank[X_BANK][:, g * P:(g + 1) * P], src[:, t, g * P:(g + 1) * P], ident[:, :])
                ins.then_inc(turned, 1)

            def score(b, p, s):
                t, g, h0, heads, keys = step_of(s)
                if s in (0, 4):
                    pe.wait_ge(turned_a, b * 4 + 2 * t + 2)
                    pe.wait_ge(turned_d, b * 2 + t + 1)
                if not (isinstance(b, int) and b * STEPS + s < 3):
                    pe.wait_ge(exp_done, b * STEPS + s - 2)
                o = bank[S_BANK[s % 3]]
                pe.matmul(o[:, :].rearrange("p (h k) -> p h k", h=heads), q_t[p][:, g, t * P:(t + 1) * P],
                          k_z[p][:, g, h0:h0 + heads, 0:keys], start=True, stop=False)
                pe.matmul(o[:, :].rearrange("p (h k) -> p h k", h=heads)[:, :, keys - P:keys], identb[:, :],
                          maskb[:, 0:heads, :], start=False, stop=True).then_inc(scored, 1)

            def turn_p(b, s):
                n = b * STEPS + s
                pe.wait_ge(exp_done, n + 1)
                if not (isinstance(b, int) and b * STEPS + s < 2):
                    if s % 2:
                        pe.wait_ge(pt_dve, b * 6 + s // 2)
                    else:
                        pe.wait_ge(pt_act, b * 6 + s // 2)
                for k in range(4):
                    ins = pe.transpose(bank[T_BANK[s % 2]][:, k * P:(k + 1) * P],
                                       prob[s % 3][:, k * P:(k + 1) * P], ident[:, :])
                ins.then_inc(p_turned, 1)

            def pv(b, p, s):
                t, g, h0, heads, keys = step_of(s)
                u = unit_of(s)
                if s in (0, 2, 4, 8) and not (isinstance(b, int) and b == 0 and s < 4):
                    pe.wait_ge(o_ready, b * 4 + u - 1)
                if s == 0:
                    pe.wait_ge(v_ready, b + 1)
                if s % 2:
                    pe.wait_ge(pt_dve, b * 6 + s // 2 + 1)
                else:
                    pe.wait_ge(pt_act, b * 6 + s // 2 + 1)
                kb = keys // P
                for h in range(heads):
                    head = 4 * g + h0 + h
                    e = (head % 8) * (HD + 1)
                    for k in range(kb):
                        c = (h * kb + k) * P
                        ins = pe.matmul(bank[O_BANK[u % 2]][:, e:e + HD + 1], prob_t[s % 3][:, c:c + P],
                                        v_a[p][:, k, head, :], start=(k == 0), stop=(k == kb - 1))
                ins.then_inc(pv_done, 1)

            for k in range(4):
                turn(0, 0, k)

            def body(b, odd=0):
                p = par(b, odd)
                more = not (isinstance(b, int) and b + 1 >= B)
                for s in range(STEPS):
                    score(b, p, s)
                    if s >= LAG_T:
                        turn_p(b, s - LAG_T)
                    elif exists(b - 1):
                        turn_p(b - 1, s - LAG_T + STEPS)
                    if s >= LAG_V:
                        pv(b, p, s - LAG_V)
                    elif exists(b - 1):
                        pv(b - 1, 1 - p, s - LAG_V + STEPS)
                    if more:
                        for k in range(4):
                            if s == TURN[k]:
                                turn(b + 1, 1 - p, k)

            batches(pe, body, B)
            turn_p(B - 1, STEPS - 2)
            pv(B - 1, 1, STEPS - 3)
            turn_p(B - 1, STEPS - 1)
            pv(B - 1, 1, STEPS - 2)
            pv(B - 1, 1, STEPS - 1)

            pe.wait_ge(o_ready, B * 4)

            def prep_turn(i, t):
                if t == 0:
                    pe.wait_ge(f_rot, i * 8 + 8)
                if exists(i - 1) or t:
                    pe.wait_ge(f_xq, i * 2 + t)
                for c in range(KC):
                    ins = pe.transpose(bank[7][:, c * P:(c + 1) * P], r_a[:, t, c, :], ident[:, :])
                ins.then_inc(f_rot_t, 1)

            def prep_had(i, t):
                pe.wait_ge(f_rot_e, i * 2 + t + 1)
                for c in range(KC):
                    ins = pe.matmul(bank[7][:, c * P:(c + 1) * P], rot_t[:, c, :], had[:, :], start=True, stop=True)
                ins.then_inc(f_had, 1)

            def prep_int(i, t):
                pe.wait_ge(f_qi, i * 2 + t + 1)
                if t == 1:
                    pe.wait_ge(f_bro, i + 1)
                for c in range(KC):
                    ins = pe.transpose(bank[7][:, 64 * c:64 * c + 64].bitcast(BF16),
                                       q_i[:, c * P:(c + 1) * P], identb[:, :])
                ins.then_inc(f_qt, 1)

            def prep_scales(i):
                pe.wait_ge(f_qi, i * 2 + 2)
                pe.wait_ge(f_diag, i * 2 + 2)
                for k in range(2):
                    ins = pe.matmul(bank[7][:, k * S:(k + 1) * S], ones[:, :],
                                    diag[:, :, :].rearrange("p t f -> p (t f)"), start=True, stop=True)
                ins.then_inc(f_brop, 1)

            def gate_up(i, p, c):
                if c == 0:
                    pe.wait_ge(f_xq, i * 2 + 2)
                if not (isinstance(i, int) and i * NP + c < 2):
                    pe.wait_ge(h_ready, i * NP + c - 1)
                for w, o in ((gate_t, bank[2 * (c % 2)]), (up_t, bank[2 * (c % 2) + 1])):
                    for h in range(2):
                        for k in range(KC):
                            f = (2 * c + h) * P
                            ins = pe.matmul(o[:, h * S:(h + 1) * S], w[:, k, f:f + P], xq_t[p][:, k, :],
                                            start=(k == 0), stop=(k == KC - 1))
                ins.then_inc(gu_done, 1)

            def transform(i, p, t, q):
                if q == 0:
                    pe.wait_ge(b4_done, i * 4 + 2 * t + 2)
                if t == 0 and q < 2:
                    if exists(i - 1):
                        pe.wait_ge(q2_ready, i * 4 - 1 + q)
                else:
                    pe.wait_ge(y_out_sem, i * 8 + 4 * t + q - 1)
                for k in range(4):
                    ins = pe.matmul(bank[4 + q % 2][:, k * P:(k + 1) * P], h_a[p][:, 4 * q + k, t * P:(t + 1) * P],
                                    had[:, :], start=True, stop=True)
                ins.then_inc(y_done, 1)

            def turn_q2(i, t, k):
                if k == 0:
                    pe.wait_ge(y_qi, i * 2 + t + 1)
                if t == 0:
                    pe.wait_ge(y_out_sem, i * 8 + 7 + k)
                else:
                    pe.wait_ge(q2_ready, i * 4 + 1 + k)
                for c in range(8):
                    ins = pe.transpose(bank[4 + k][:, 64 * c:64 * c + 64].bitcast(BF16),
                                       q2_i[:, t, (8 * k + c) * P:(8 * k + c + 1) * P], identb[:, :])
                ins.then_inc(q2_turned, 1)

            def down(i, t):
                pe.wait_ge(q2_ready, i * 4 + 2 * t + 2)
                if not (isinstance(i, int) and i == 0 and t == 0):
                    pe.wait_ge(o2_ready, i * 2 + t)
                for c in range(NC):
                    ins = pe.matmul(bank[6][:, :], q2_t[:, t, c, :], down_t[:, c, :],
                                    start=(c == 0), stop=(c == NC - 1))
                ins.then_inc(d_done, 1)

            for t in range(TT):
                prep_turn(0, t)
                prep_had(0, t)
                if t == 1:
                    prep_scales(0)
                prep_int(0, t)

            def body2(i, odd=0):
                p = par(i, odd)
                here, before, two, ahead = exists(i, B), exists(i - 1, B), exists(i - 2, B), exists(i + 1, B)
                for c in range(NP):
                    if here:
                        gate_up(i, p, c)
                    if c == 0 and two:
                        turn_q2(i - 2, 0, 0)
                        turn_q2(i - 2, 0, 1)
                    if c == 0 and ahead:
                        prep_turn(i + 1, 0)
                    if c == 1 and ahead:
                        prep_had(i + 1, 0)
                    if c == 1 and two:
                        down(i - 2, 0)
                    if c == 2 and two:
                        turn_q2(i - 2, 1, 0)
                        turn_q2(i - 2, 1, 1)
                    if c == 2 and ahead:
                        prep_int(i + 1, 0)
                    if c == 3 and ahead:
                        prep_turn(i + 1, 1)
                    if c == 3 and two:
                        down(i - 2, 1)
                    if c == 4 and ahead:
                        prep_had(i + 1, 1)
                    if c >= 4 and before:
                        for q in (2 * (c - 4), 2 * (c - 4) + 1):
                            transform(i - 1, 1 - p, q // 4, q % 4)
                    if c == 5 and ahead:
                        prep_scales(i + 1)
                    if c == 6 and ahead:
                        prep_int(i + 1, 1)

            batches(pe, body2, B)
            body2(B)
            body2(B + 1)


def kernel(**inputs):
    import concourse.bacc as bacc
    from concourse.bass_utils import run_bass_kernel_spmd

    bits = np.array([[bin(a & b).count("1") for b in range(P)] for a in range(P)])
    arrays = {name: np.ascontiguousarray(inputs[name]) for name in
              ("x", "ctx_2048", "L0_ffn_w_gate", "L0_ffn_w_up", "L0_ffn_w_down")}
    arrays["identity"] = np.eye(P, dtype=np.float32)
    arrays["hadamard"] = (1 - 2 * (bits % 2)).astype(np.float32)
    arrays["causal"] = np.triu(np.full((P, P), MASKED, np.float32), 1)
    nc = bacc.Bacc("TRN2", target_bir_lowering=False, num_devices=1)
    args = [nc.dram_tensor(name, a.shape, mybir.dt.from_np(a.dtype), kind="ExternalInput").ap()
            for name, a in arrays.items()]
    shape = arrays["x"].shape
    args.append(nc.dram_tensor("out", shape, F32, kind="ExternalOutput").ap())
    attention_ffn(nc, *args)
    result = run_bass_kernel_spmd(nc, [arrays], core_ids=[0])
    return result.results[0]["out"]
```

```python
from contextlib import ExitStack

import numpy as np

import concourse.bass as bass
from concourse import mybir

F32 = mybir.dt.float32
BF16 = mybir.dt.bfloat16
ALU = mybir.AluOpType
ACT = mybir.ActivationFunctionType
AX = mybir.AxisListType

P = 128
NHEADS = 16
HD = 32
GROUPS = 4
EPS = 1e-5
ROUND = 12582912.0
MASKED = -1e38
STEPS = 12
LAG_T, LAG_V = 2, 3
TURN = (6, 8, 10, 12)
UNIT_END = (1, 3, 7, 11)
FINAL = (5, 7, 11, 14)


def exists(i, count=1 << 30):
    return not isinstance(i, int) or 0 <= i < count


def attention_ffn(nc, x, ctx, w_gate, w_up, w_down, ident_in, had_in, mask_in, out):
    B, S, D = x.shape
    FF = w_gate.shape[0]
    NC = FF // P
    KC = D // P
    TT = S // P
    NP = NC // 2
    WT = FF * D // P // D

    es = ExitStack()
    with es:
        def sb(name, shape, dt=F32):
            return es.enter_context(nc.sbuf_tensor(name, shape, dt))

        def sem(name):
            return es.enter_context(nc.semaphore(name))

        bank = [es.enter_context(nc.psum_tensor(f"bank{i}", [P, 512], F32)) for i in range(8)]

        ident = sb("ident", [P, P])
        had = sb("had", [P, P])
        ones = sb("ones", [P, P])
        maskf = sb("maskf", [P, P])
        identb = sb("identb", [P, P], BF16)
        maskb = sb("maskb", [P, 4, P], BF16)
        gate_t = sb("gate_t", [P, KC, FF], BF16)
        up_t = sb("up_t", [P, KC, FF], BF16)
        down_t = sb("down_t", [P, NC, D], BF16)
        wsum = sb("wsum", [P, 3, WT])
        wcol = sb("wcol", [P, 3])
        wscale = sb("wscale", [P, 3])
        wthr = sb("wthr", [P, 3])
        wnthr = sb("wnthr", [P, 3])
        rnd = sb("rnd", [P, 1])
        nhalf = sb("nhalf", [P, TT])
        arena = sb("arena", [P, 29 * 1024])
        wf = arena[:, 0:3 * WT * D].rearrange("p (m t n) -> p m t n", m=3, t=WT)
        tern = sb("tern", [P, WT, D], BF16)
        below = arena[:, 3 * WT * D:3 * WT * D + WT * D // 2].bitcast(BF16).rearrange("p (t n) -> p t n", t=WT)

        at = [0]

        def piece(words, pattern=None, **dims):
            a = arena[:, at[0]:at[0] + words]
            at[0] += words
            return a.rearrange(pattern, **dims) if pattern else a

        x_in = [piece(TT * D, "p (t d) -> p t d", t=TT) for _ in range(2)]
        c_in = [piece(TT * D, "p (t d) -> p t d", t=TT) for _ in range(2)]
        xn = [piece(TT * D, "p (t d) -> p t d", t=TT) for _ in range(2)]
        q_t = [piece(GROUPS * S, "p (g s) -> p g s", g=GROUPS) for _ in range(2)]
        k_z = [piece(GROUPS * 4 * S, "p (g h s) -> p g h s", g=GROUPS, h=4) for _ in range(2)]
        v_a = [piece(TT * NHEADS * (HD + 1), "p (t h e) -> p t h e", t=TT, h=NHEADS) for _ in range(2)]
        x_add = piece(TT * D, "p (t d) -> p t d", t=TT)
        prob = [piece(512) for _ in range(3)]
        prob_t = [piece(512) for _ in range(3)]
        o_sb = [piece(TT * D, "p (t d) -> p t d", t=TT) for _ in range(2)]
        used_1 = at[0]
        at[0] = 0
        h_a = [piece(NC * S, "p (c s) -> p c s", c=NC) for _ in range(2)]
        h_b = [piece(NC * S, "p (c s) -> p c s", c=NC) for _ in range(2)]
        y_sb = [piece(FF) for _ in range(TT)]
        x1 = [piece(TT * D, "p (t d) -> p t d", t=TT) for _ in range(2)]
        x_res = [piece(TT * D, "p (t d) -> p t d", t=TT) for _ in range(2)]
        r_a = piece(TT * D, "p (t c f) -> p t c f", t=TT, c=KC)
        r_b = piece(TT * D, "p (t c f) -> p t c f", t=TT, c=KC)
        z_sb = [piece(512) for _ in range(2)]
        s_sb = [piece(512) for _ in range(2)]
        bro = [piece(2 * S) for _ in range(2)]
        assert max(at[0], used_1) <= 29 * 1024, (at[0], used_1)
        rot_t = sb("rot_t", [P, KC, P])
        qm = sb("qm", [P, D])
        q_i = sb("q_i", [P, D], BF16)
        xq_t = [sb(f"xq_t{n}", [P, KC, S], BF16) for n in range(2)]
        q2_i = tern[:, 0:TT * 4, :].rearrange("p (t c) n -> p t (c n)", t=TT)
        q2_t = tern[:, TT * 4:2 * TT * 4, :].rearrange("p (t c) n -> p t (c n)", t=TT).rearrange(
            "p t (c n) -> p t c n", n=P)
        y_out = [sb(f"y_out{n}", [P, D]) for n in range(TT)]
        diag = sb("diag", [P, TT, P])
        bn = sb("bn", [P, TT, 6])
        mv = sb("mv", [P, TT, 2])
        vareps = sb("vareps", [P, TT])
        rstd = sb("rstd", [P, TT])
        rstd_s = sb("rstd_s", [P, TT])
        nmax = sb("nmax", [P, STEPS, 4])
        rinv = sb("rinv", [P, 4, 8])
        nmean = sb("nmean", [P, TT])
        amax = sb("amax", [P, TT])
        m1 = sb("m1", [P, TT])
        r1 = sb("r1", [P, TT])
        qs1 = sb("qs1", [P, TT])
        cg = sb("cg", [P, TT])
        ku = [sb(f"ku{n}", [P, TT]) for n in range(4)]
        amax2 = sb("amax2", [P, TT])
        m2 = sb("m2", [P, TT])
        r2 = sb("r2", [P, TT])
        qs2 = sb("qs2", [P, TT])
        dd = [sb(f"dd{n}", [P, TT]) for n in range(2)]

        const_in = sem("const_in")
        const_ok = sem("const_ok")
        w_in = [sem(f"w_in{m}") for m in range(3)]
        w_summed = sem("w_summed")
        w_total = sem("w_total")
        w_chain = sem("w_chain")
        w_below = sem("w_below")
        w_tern = sem("w_tern")
        w_turned = sem("w_turned")
        w_out_d = sem("w_out_d")
        w_out_a = sem("w_out_a")
        x_loaded = [sem(f"x_loaded{n}") for n in range(2)]
        c_loaded = [sem(f"c_loaded{n}") for n in range(2)]
        zeroed = sem("zeroed")
        ln_chain = sem("ln_chain")
        var_ready = sem("var_ready")
        rstd_ready = sem("rstd_ready")
        xn_ready = sem("xn_ready")
        v_ready = sem("v_ready")
        turned = sem("turned")
        turned_a = sem("turned_a")
        turned_d = sem("turned_d")
        scored = sem("scored")
        max_ready = sem("max_ready")
        exp_done = sem("exp_done")
        p_turned = sem("p_turned")
        pt_act = sem("pt_act")
        pt_dve = sem("pt_dve")
        pv_done = sem("pv_done")
        rinv_ready = sem("rinv_ready")
        o_ready = sem("o_ready")
        x_again = [[sem(f"x_again{t}{n}") for n in range(2)] for t in range(TT)]
        x1_ready = sem("x1_ready")
        x1_stored = [sem(f"x1_stored{n}") for n in range(2)]
        f_loaded = [sem(f"f_loaded{n}") for n in range(2)]
        r_loaded = [sem(f"r_loaded{n}") for n in range(2)]
        f_ln = sem("f_ln")
        f_var = sem("f_var")
        f_rstd = sem("f_rstd")
        f_nb = sem("f_nb")
        f_xn = sem("f_xn")
        f_rot = sem("f_rot")
        f_rot_t = sem("f_rot_t")
        f_rot_e = sem("f_rot_e")
        f_had = sem("f_had")
        f_stat = sem("f_stat")
        f_qs = sem("f_qs")
        f_qm = sem("f_qm")
        f_qi = sem("f_qi")
        f_qt = sem("f_qt")
        f_xq = sem("f_xq")
        f_diag = sem("f_diag")
        f_brop = sem("f_brop")
        f_bro = sem("f_bro")
        gu_done = sem("gu_done")
        z_ready = sem("z_ready")
        s_ready = sem("s_ready")
        h_ready = sem("h_ready")
        b1_done = sem("b1_done")
        b2_done = sem("b2_done")
        b3_done = sem("b3_done")
        b4_done = sem("b4_done")
        y_done = sem("y_done")
        y_out_sem = sem("y_evac")
        y_stat = sem("y_stat")
        y_qs = sem("y_qs")
        dd_ready = sem("dd_ready")
        y_qm = sem("y_qm")
        y_qi = sem("y_qi")
        q2_turned = sem("q2_turned")
        q2_ready = sem("q2_ready")
        d_done = sem("d_done")
        o2_ready = sem("o2_ready")
        stored = [sem(f"stored{n}") for n in range(TT)]

        block = es.enter_context(nc.Block())

        weights = (w_gate, w_up, w_down)
        weights_t = (gate_t, up_t, down_t)

        def w_blocks(m, t):
            if m < 2:
                return weights_t[m][:, :, t * P:(t + 1) * P]
            a, b = t // (FF // D), t % (FF // D)
            return down_t[:, b * KC:(b + 1) * KC, a * P:(a + 1) * P]

        S_BANK, T_BANK, O_BANK, X_BANK = (0, 1, 2), (3, 4), (5, 6), 7

        def step_of(s):
            if s < GROUPS:
                return 0, s, 0, 4, P
            return 1, (s - GROUPS) // 2, 2 * ((s - GROUPS) % 2), 2, S

        def unit_of(s):
            t, g, _, _, _ = step_of(s)
            return 2 * t + g // 2

        def batches(engine, body, count, last=2):
            body(0)
            body(1)
            with engine.Fori(1, (count - last) // 2) as j:
                body(j * 2)
                body(j * 2 + 1, 1)
            for i in range(count - last, count):
                body(i)

        def quads(engine, body, count):
            for i in range(4):
                body(i, i)
            with engine.Fori(1, count // 4 - 1) as j:
                for q in range(4):
                    body(j * 4 + q, q)
            for i in range(count - 4, count):
                body(i, i % 4)

        def par(i, odd):
            return i % 2 if isinstance(i, int) else odd

        @block.sync
        def _(sp):
            for dst, src in ((ident, ident_in), (had, had_in), (maskf, mask_in)):
                sp.dma_start(dst[:, :], src).then_inc(const_in, 16)
            for m in range(2):
                sp.dma_start(wf[:, m, :, :], weights[m].rearrange("(t p) n -> p t n", p=P)).then_inc(w_in[m], 16)
            for a in range(D // P):
                sp.dma_start(wf[:, 2, a * KC:(a + 1) * KC, :].rearrange("p b n -> p (b n)"),
                             w_down[a * P:(a + 1) * P, :]).then_inc(w_in[2], 16)

            def load(b, p):
                sp.dma_start(x_in[p], x[b:b + 1].rearrange("o (t p) d -> p (o t) d", p=P)
                             if isinstance(b, int) else
                             x[bass.ds(b, 1)].rearrange("o (t p) d -> p (o t) d", p=P)
                             ).then_inc(x_loaded[p], 16)
                sp.dma_start(c_in[p], ctx[b:b + 1].rearrange("o (t p) d -> p (o t) d", p=P)
                             if isinstance(b, int) else
                             ctx[bass.ds(b, 1)].rearrange("o (t p) d -> p (o t) d", p=P)
                             ).then_inc(c_loaded[p], 16)

            def load_add(b, p, t):
                rows = x.rearrange("b s d -> (b s) d")
                at_row = b * S + t * P
                sp.dma_start(x_add[:, t, :], rows[at_row:at_row + P, :] if isinstance(b, int) else
                             rows[bass.ds(at_row, P), :]
                             ).then_inc(x_again[t][p], 16)

            def store_1(b, p):
                sp.wait_ge(x1_ready, b * TT + TT)
                dst = out[b:b + 1] if isinstance(b, int) else out[bass.ds(b, 1)]
                sp.dma_start(dst.rearrange("o (t p) d -> p (o t) d", p=P), o_sb[p]).then_inc(x1_stored[p], 16)

            def next_add(b, p, t):
                if exists(b, B):
                    if exists(b - 1):
                        sp.wait_ge(x1_ready, b * TT - TT + t + 1)
                    load_add(b, p, t)

            def next_load(b, p):
                sp.wait_ge(xn_ready, b * 2 - 2)
                sp.wait_ge(v_ready, b - 1)
                sp.wait_ge(turned, b * 4 - 4)
                load(b, p)

            sp.wait_ge(w_tern, 3)
            load(0, 0)
            next_add(0, 0, 0)
            load(1, 1)
            next_add(0, 0, 1)
            next_add(1, 1, 0)
            next_load(2, 0)

            def batch_1(b, odd=0):
                p = par(b, odd)
                store_1(b, p)
                next_add(b + 1, 1 - p, 1)
                next_add(b + 2, p, 0)
                if exists(b + 3, B):
                    next_load(b + 3, 1 - p)

            batches(sp, batch_1, B, last=4)

            def load_2(i, p):
                src = out[i:i + 1] if isinstance(i, int) else out[bass.ds(i, 1)]
                sp.dma_start(x1[p], src.rearrange("o (t p) d -> p (o t) d", p=P)).then_inc(f_loaded[p], 16)

            def load_res(i, p):
                src = out[i:i + 1] if isinstance(i, int) else out[bass.ds(i, 1)]
                sp.dma_start(x_res[p], src.rearrange("o (t p) d -> p (o t) d", p=P)).then_inc(r_loaded[p], 16)

            for p in range(2):
                sp.wait_ge(x1_stored[p], 16 * (B // 2))
            load_2(0, 0)
            load_2(1, 1)

            def store_2(i, odd=0):
                for t in range(TT):
                    sp.wait_ge(o2_ready, i * TT + t + 1)
                    rows = (out[i:i + 1] if isinstance(i, int) else out[bass.ds(i, 1)])
                    sp.dma_start(rows[:, t * P:(t + 1) * P, :].rearrange("o p d -> p (o d)"),
                                 y_out[t][:, :]).then_inc(stored[t], 16)

            def quad(i, q):
                p = q % 2
                if not (isinstance(i, int) and i + 2 >= B):
                    sp.wait_ge(f_xn, i * 2 + 2)
                    load_2(i + 2, p)
                if exists(i - 2):
                    store_2(i - 2, p)
                load_res(i, p)

            quads(sp, quad, B)
            for i in range(B, B + 2):
                store_2(i - 2)
            for t in range(TT):
                sp.wait_ge(stored[t], 16 * B)

        @block.gpsimd
        def _(pool):
            pool.memset(ones[:, :], 1.0).then_inc(const_ok, 1)
            pool.memset(rnd[:, :], ROUND).then_inc(const_ok, 1)
            pool.memset(nhalf[:, :], -0.5).then_inc(const_ok, 1)
            pool.wait_ge(w_tern, 3)
            for p in range(2):
                pool.memset(k_z[p], 0.0).then_inc(zeroed, 1)
                pool.memset(v_a[p], 1.0).then_inc(zeroed, 1)
            pool.wait_ge(zeroed, 4)

            def prepare(b, p):
                pool.wait_ge(c_loaded[p], (b // 2) * 16 + 16 if isinstance(b, int) else (b - p) * 8 + 16)
                if exists(b - 2):
                    pool.wait_ge(pv_done, b * STEPS - STEPS)
                pool.wait_ge(var_ready, b + 1)
                pool.tensor_tensor(rstd[:, :], vareps[:, :], nhalf[:, :], ALU.pow).then_inc(rstd_ready, 1)
                pool.tensor_copy(v_a[p][:, :, :, 0:HD],
                                 c_in[p].rearrange("p t (h e) -> p t h e", e=HD)).then_inc(v_ready, 1)

            def residual(b, p, t):
                pool.wait_ge(x_again[t][p], (b // 2) * 16 + 16 if isinstance(b, int) else (b - p) * 8 + 16)
                pool.wait_ge(o_ready, b * 4 + 2 * t + 2)
                pool.tensor_tensor(o_sb[p][:, t, :], o_sb[p][:, t, :], x_add[:, t, :],
                                   ALU.add).then_inc(x1_ready, 1)

            prepare(0, 0)

            def body(b, odd=0):
                p = par(b, odd)
                if not (isinstance(b, int) and b + 1 >= B):
                    prepare(b + 1, 1 - p)
                if exists(b - 1):
                    residual(b - 1, 1 - p, 1)
                residual(b, p, 0)

            batches(pool, body, B)
            residual(B - 1, 1, 1)

            def rotate(i, p):
                pool.wait_ge(f_var, i + 1)
                pool.tensor_tensor(rstd[:, :], vareps[:, :], nhalf[:, :], ALU.pow).then_inc(f_rstd, 1)
                pool.wait_ge(f_xn, i * 2 + 2)
                a = r_a.rearrange("p t (u v) f -> p t u v f", v=2)
                b_ = r_b.rearrange("p t (u v) f -> p t u v f", v=2)
                for t in range(TT):
                    pool.tensor_tensor(b_[:, t, :, 0, :], a[:, t, :, 0, :], a[:, t, :, 1, :], ALU.add).then_inc(f_rot, 1)
                    pool.tensor_tensor(b_[:, t, :, 1, :], a[:, t, :, 0, :], a[:, t, :, 1, :], ALU.subtract).then_inc(f_rot, 1)
                pool.wait_ge(f_rot, i * 8 + 4)
                for t in range(TT):
                    pool.tensor_tensor(r_a[:, t, 0:2, :], r_b[:, t, 0:2, :], r_b[:, t, 2:4, :], ALU.add).then_inc(f_rot, 1)
                    pool.tensor_tensor(r_a[:, t, 2:4, :], r_b[:, t, 0:2, :], r_b[:, t, 2:4, :], ALU.subtract).then_inc(f_rot, 1)

            def stages(i, p, which):
                a, b_ = h_a[p], h_b[p]
                for g in which:
                    lo = 4 * g
                    pool.wait_ge(b1_done, i * 8 + 2 * g + 2)
                    pool.tensor_tensor(a[:, lo:lo + 2, :], b_[:, lo:lo + 2, :], b_[:, lo + 2:lo + 4, :], ALU.add).then_inc(b2_done, 1)
                    pool.tensor_tensor(a[:, lo + 2:lo + 4, :], b_[:, lo:lo + 2, :], b_[:, lo + 2:lo + 4, :], ALU.subtract).then_inc(b2_done, 1)
                    if g % 2 == 1:
                        lo -= 4
                        pool.wait_ge(b2_done, i * 8 + 2 * g + 2)
                        pool.tensor_tensor(b_[:, lo:lo + 4, :], a[:, lo:lo + 4, :], a[:, lo + 4:lo + 8, :], ALU.add).then_inc(b3_done, 1)
                        pool.tensor_tensor(b_[:, lo + 4:lo + 8, :], a[:, lo:lo + 4, :], a[:, lo + 4:lo + 8, :], ALU.subtract).then_inc(b3_done, 1)
                    if g == 3:
                        pool.wait_ge(b3_done, i * 4 + 4)
                        for t in range(TT):
                            c = slice(t * P, (t + 1) * P)
                            pool.tensor_tensor(a[:, 0:8, c], b_[:, 0:8, c], b_[:, 8:16, c], ALU.add).then_inc(b4_done, 1)
                            pool.tensor_tensor(a[:, 8:16, c], b_[:, 0:8, c], b_[:, 8:16, c], ALU.subtract).then_inc(b4_done, 1)

            rotate(0, 0)
            rotate(1, 1)

            def body2(i, odd=0):
                p = par(i, odd)
                if exists(i - 1):
                    stages(i - 1, 1 - p, (3,))
                if exists(i, B):
                    stages(i, p, (0, 1))
                if exists(i + 2, B):
                    rotate(i + 2, p)
                if exists(i, B):
                    stages(i, p, (2,))

            batches(pool, body2, B)
            body2(B)

        @block.scalar
        def _(act):
            for n in range(3 * WT // 2):
                if n % 2 == 1:
                    m, t = divmod(2 * n, WT)
                    act.wait_ge(w_turned, n + 1)
                    for k in range(2):
                        ins = act.activation(
                            w_blocks(m, t + k),
                            bank[n % 4][:, :].bitcast(BF16).rearrange("p (k c f) -> p k c f", k=2, c=KC)[:, k],
                            ACT.Copy)
                    ins.then_inc(w_out_a, 1)

            def softmax(b, p, s):
                _, _, _, heads, keys = step_of(s)
                n = b * STEPS + s
                act.wait_ge(max_ready, n + 1)
                if not (isinstance(b, int) and b * STEPS + s < 3):
                    act.wait_ge(p_turned, n - 2)
                for h in range(heads):
                    ins = act.activation(prob[s % 3][:, h * keys:(h + 1) * keys],
                                         bank[S_BANK[s % 3]][:, h * keys:(h + 1) * keys],
                                         ACT.Exp, bias=nmax[:, s, h:h + 1])
                ins.then_inc(exp_done, 1)

            def out_pt(b, s):
                n = b * STEPS + s
                act.wait_ge(p_turned, n + 1)
                if not (isinstance(b, int) and b * STEPS + s < 3):
                    act.wait_ge(pv_done, n - 2)
                act.activation(prob_t[s % 3], bank[T_BANK[s % 2]][:, :], ACT.Copy).then_inc(pt_act, 1)

            def out_turn(b, p, k):
                t = k // 2
                act.wait_ge(turned, b * 4 + k + 1)
                src = bank[X_BANK][:, :].rearrange("p (g s) -> p g s", g=GROUPS)
                if k % 2 == 0:
                    act.activation(q_t[p][:, :, t * P:(t + 1) * P], src, ACT.Copy).then_inc(turned_a, 1)
                else:
                    for h in range(2):
                        r = slice(h * HD, (h + 1) * HD)
                        ins = act.activation(k_z[p][r, :, h, t * P:(t + 1) * P], src[r], ACT.Copy)
                    ins.then_inc(turned_a, 1)

            act.wait_ge(zeroed, 4)
            for k in range(3):
                out_turn(0, 0, k)

            def body(b, odd=0):
                p = par(b, odd)
                more = not (isinstance(b, int) and b + 1 >= B)
                for s in range(STEPS):
                    softmax(b, p, s)
                    if s % 2 == 0 and (s >= 2 or exists(b - 1)):
                        out_pt(b if s >= 2 else b - 1, (s - 2) % STEPS)
                    for k in range(4):
                        if s == TURN[k] + 1 and more:
                            out_turn(b + 1, 1 - p, k)
                        if s == TURN[k] + 1 - STEPS:
                            out_turn(b, p, k)

            batches(act, body, B)
            out_pt(B - 1, STEPS - 2)

            def normalise(i, p):
                if exists(i - 1):
                    act.wait_ge(f_rot_t, i * 2)
                act.wait_ge(f_nb, i + 1)
                for t in range(TT):
                    act.activation(r_a[:, t, :, :].rearrange("p c f -> p (c f)"), x1[p][:, t, :],
                                   ACT.Identity, scale=rstd[:, t:t + 1], bias=nmean[:, t:t + 1]).then_inc(f_xn, 1)

            def prep_turn(i, t):
                act.wait_ge(f_rot_t, i * 2 + t + 1)
                act.activation(rot_t[:, :, :], bank[7][:, :].rearrange("p (c f) -> p c f", c=KC),
                               ACT.Copy).then_inc(f_rot_e, 1)

            def prep_round(i, t):
                act.wait_ge(f_qs, i * 2 + t + 1)
                act.activation(qm[:, :], bank[7][:, :], ACT.Identity, scale=qs1[:, t:t + 1],
                               bias=rnd[:, 0:1]).then_inc(f_qm, 1)

            def prep_xq(i, p, t):
                act.wait_ge(f_qt, i * 2 + t + 1)
                act.activation(xq_t[p][:, :, t * P:(t + 1) * P],
                               bank[7][:, 0:D // 2].bitcast(BF16).rearrange("p (c f) -> p c f", c=KC),
                               ACT.Copy).then_inc(f_xq, 1)

            def prep_bro(i, p):
                act.wait_ge(f_brop, i + 1)
                act.activation(bro[p], bank[7][:, :], ACT.Copy).then_inc(f_bro, 1)

            def silu(i, c):
                act.wait_ge(z_ready, i * NP + c + 1)
                act.activation(s_sb[c % 2], z_sb[c % 2], ACT.Silu).then_inc(s_ready, 1)

            def out_y(i, t, q):
                act.wait_ge(y_done, i * 8 + 4 * t + q + 1)
                act.activation(y_sb[t][:, q * 512:(q + 1) * 512], bank[4 + q % 2][:, :],
                               ACT.Copy).then_inc(y_out_sem, 1)

            def round_y(i, t):
                act.wait_ge(y_qs, i * 2 + t + 1)
                act.activation(y_sb[t], y_sb[t], ACT.Identity, scale=qs2[:, t:t + 1],
                               bias=rnd[:, 0:1]).then_inc(y_qm, 1)

            def out_q2(i, t, k):
                act.wait_ge(q2_turned, i * 4 + 2 * t + k + 1)
                act.activation(q2_t[:, t, 8 * k:8 * k + 8, :],
                               bank[4 + k][:, :].bitcast(BF16).rearrange("p (c f) -> p c f", c=8),
                               ACT.Copy).then_inc(q2_ready, 1)

            normalise(0, 0)
            for t in range(TT):
                prep_turn(0, t)
                prep_round(0, t)
                if t == 1:
                    prep_bro(0, 0)
                prep_xq(0, 0, t)
            normalise(1, 1)
            prep_turn(1, 0)

            def body2(i, q):
                p = q % 2
                here, before, two, ahead = exists(i, B), exists(i - 1, B), exists(i - 2, B), exists(i + 1, B)
                for c in range(NP):
                    if here:
                        silu(i, c)
                    if c == 0 and two:
                        out_q2(i - 2, 0, 0)
                        out_q2(i - 2, 0, 1)
                    if c == 1 and ahead:
                        prep_round(i + 1, 0)
                    if c == 1 and two:
                        round_y(i - 2, 1)
                    if c == 2 and ahead:
                        prep_xq(i + 1, 1 - p, 0)
                    if c == 2 and two:
                        out_q2(i - 2, 1, 0)
                        out_q2(i - 2, 1, 1)
                    if c == 3 and ahead:
                        prep_turn(i + 1, 1)
                    if c == 5 and exists(i + 2, B):
                        normalise(i + 2, p)
                    if c == 5 and ahead:
                        prep_round(i + 1, 1)
                    if c == 6 and ahead:
                        prep_bro(i + 1, 1 - p)
                    if 3 <= c < 7 and before:
                        for k in (2 * (c - 3), 2 * (c - 3) + 1):
                            out_y(i - 1, k // 4, k % 4)
                    if c == 6 and ahead:
                        prep_xq(i + 1, 1 - p, 1)
                    if c == 7 and before:
                        round_y(i - 1, 0)
                    if c == 7 and exists(i + 2, B):
                        prep_turn(i + 2, 0)

            quads(act, body2, B)
            body2(B, 0)
            body2(B + 1, 1)

        @block.vector
        def _(dve):
            dve.wait_ge(const_in, 48)
            dve.tensor_copy(identb[:, :], ident[:, :]).then_inc(const_ok, 1)
            for h in range(4):
                ins = dve.tensor_copy(maskb[:, h, :], maskf[:, :])
            ins.then_inc(const_ok, 1)
            chain = 0
            for m in range(3):
                dve.wait_ge(w_in[m], 64 if m == 2 else 16)
                dve.tensor_reduce(wsum[:, m, :], wf[:, m, :, :], AX.X, ALU.add,
                                  apply_absolute_value=True).then_inc(w_chain, 1)
                chain += 1
                dve.wait_ge(w_chain, chain)
                dve.tensor_reduce(wcol[:, m:m + 1], wsum[:, m, :], AX.X, ALU.add).then_inc(w_summed, 1)
                dve.wait_ge(w_total, m + 1)
                dve.tensor_scalar(wscale[:, m:m + 1], bank[4][:, m:m + 1], 1.0 / (FF * D), EPS,
                                  ALU.mult, ALU.max).then_inc(w_chain, 1)
                chain += 1
                dve.wait_ge(w_chain, chain)
                dve.tensor_scalar(wthr[:, m:m + 1], wscale[:, m:m + 1], 0.5, None, ALU.mult).then_inc(w_chain, 1)
                dve.tensor_scalar(wnthr[:, m:m + 1], wscale[:, m:m + 1], -0.5, None, ALU.mult).then_inc(w_chain, 1)
                chain += 2
                dve.wait_ge(w_chain, chain)
                dve.tensor_scalar(below, wf[:, m, :, :], wnthr[:, m:m + 1], None, ALU.is_lt).then_inc(w_chain, 1)
                chain += 1
                dve.wait_ge(w_chain, chain)
                if m:
                    dve.wait_ge(w_turned, m * WT // 2)
                dve.scalar_tensor_tensor(out=tern[:, :, :], in0=wf[:, m, :, :], scalar=wthr[:, m:m + 1],
                                         in1=below, op0=ALU.is_gt, op1=ALU.subtract).then_inc(w_tern, 1)
                for n in range(m * WT // 2, (m + 1) * WT // 2):
                    if n % 2 == 0:
                        t = 2 * n - m * WT
                        dve.wait_ge(w_turned, n + 1)
                        for k in range(2):
                            ins = dve.tensor_copy(
                                w_blocks(m, t + k),
                                bank[n % 4][:, :].bitcast(BF16).rearrange("p (k c f) -> p k c f", k=2, c=KC)[:, k])
                        ins.then_inc(w_out_d, 1)

            def moments(b, src, chain_sem, per):
                for t in range(TT):
                    dve.bn_stats(bn[:, t, :], src[:, t, :]).then_inc(chain_sem, 1)
                dve.wait_ge(chain_sem, b * per + 2)
                dve.memset(vareps[:, :], 0.0).then_inc(chain_sem, 1)
                for t in range(TT):
                    dve.bn_aggr(mv[:, t, :], bn[:, t, :]).then_inc(chain_sem, 1)
                dve.wait_ge(chain_sem, b * per + 5)

            def norm_1(b, p):
                dve.wait_ge(x_loaded[p], (b // 2) * 16 + 16 if isinstance(b, int) else (b - p) * 8 + 16)
                moments(b, x_in[p], ln_chain, 6)
                dve.tensor_scalar(vareps[:, :], mv[:, :, 1], EPS, None, ALU.add).then_inc(var_ready, 1)

            def norm_2(b, p):
                dve.wait_ge(rstd_ready, b + 1)
                dve.tensor_scalar(rstd_s[:, :], rstd[:, :], float(HD) ** -0.5, None, ALU.mult).then_inc(ln_chain, 1)
                dve.wait_ge(ln_chain, b * 6 + 6)
                for t in range(TT):
                    dve.tensor_scalar(xn[p][:, t, :], x_in[p][:, t, :], mv[:, t, 0:1], rstd_s[:, t:t + 1],
                                      ALU.subtract, ALU.mult).then_inc(xn_ready, 1)

            def out_turn(b, p, k):
                t = k // 2
                dve.wait_ge(turned, b * 4 + k + 1)
                src = bank[X_BANK][:, :].rearrange("p (g s) -> p g s", g=GROUPS)
                for h in range(2, 4):
                    r = slice(h * HD, (h + 1) * HD)
                    ins = dve.tensor_copy(k_z[p][r, :, h, t * P:(t + 1) * P], src[r])
                ins.then_inc(turned_d, 1)

            def row_max(b, s):
                _, _, _, heads, keys = step_of(s)
                dve.wait_ge(scored, b * STEPS + s + 1)
                dve.tensor_reduce(nmax[:, s, 0:heads],
                                  bank[S_BANK[s % 3]][:, :].rearrange("p (h k) -> p h k", h=heads),
                                  AX.X, ALU.max, negate=True).then_inc(max_ready, 1)

            def out_pt(b, s):
                n = b * STEPS + s
                dve.wait_ge(p_turned, n + 1)
                if not (isinstance(b, int) and b * STEPS + s < 3):
                    dve.wait_ge(pv_done, n - 2)
                dve.tensor_copy(prob_t[s % 3], bank[T_BANK[s % 2]][:, :]).then_inc(pt_dve, 1)

            def final(b, p, u):
                t, half = divmod(u, 2)
                dve.wait_ge(pv_done, b * STEPS + UNIT_END[u] + 1)
                o = bank[O_BANK[u % 2]][:, 0:8 * (HD + 1)].rearrange("p (h e) -> p h e", h=8)
                dve.reciprocal(rinv[:, u, :], o[:, :, HD]).then_inc(rinv_ready, 1)
                dve.wait_ge(rinv_ready, b * 4 + u + 1)
                if exists(b - 2) and u == 0:
                    dve.wait_ge(x1_stored[p], (b // 2) * 16 if isinstance(b, int) else (b - p) * 8)
                dve.tensor_tensor(o_sb[p][:, t, half * 256:(half + 1) * 256].rearrange("p (h e) -> p h e", h=8),
                                  o[:, :, 0:HD], rinv[:, u, :].unsqueeze(2).to_broadcast([P, 8, HD]),
                                  ALU.mult).then_inc(o_ready, 1)

            dve.wait_ge(zeroed, 4)
            norm_1(0, 0)
            norm_2(0, 0)
            out_turn(0, 0, 1)

            def body(b, odd=0):
                p = par(b, odd)
                more = not (isinstance(b, int) and b + 1 >= B)
                for s in range(STEPS):
                    row_max(b, s)
                    if s % 2 == 1 and (s >= 2 or exists(b - 1)):
                        out_pt(b if s >= 2 else b - 1, (s - 2) % STEPS)
                    for u in range(3):
                        if s == FINAL[u]:
                            final(b, p, u)
                    if s == FINAL[3] - STEPS and exists(b - 1):
                        final(b - 1, 1 - p, 3)
                    if more:
                        if s == 2:
                            norm_1(b + 1, 1 - p)
                        if s == 4:
                            norm_2(b + 1, 1 - p)
                        if s == TURN[1] + 1:
                            out_turn(b + 1, 1 - p, 1)
                    if s == TURN[3] + 1 - STEPS:
                        out_turn(b, p, 3)

            batches(dve, body, B)
            out_pt(B - 1, STEPS - 1)
            final(B - 1, 1, 3)

            def f_norm(i, p):
                dve.wait_ge(f_loaded[p], (i // 2) * 16 + 16 if isinstance(i, int) else (i - p) * 8 + 16)
                if exists(i - 1):
                    dve.wait_ge(f_xn, i * 2)
                moments(i, x1[p], f_ln, 5)
                dve.tensor_scalar(vareps[:, :], mv[:, :, 1], EPS, None, ALU.add).then_inc(f_var, 1)

            def f_shift(i):
                dve.wait_ge(f_rstd, i + 1)
                dve.scalar_tensor_tensor(out=nmean[:, :], in0=mv[:, :, 0], scalar=-1.0, in1=rstd[:, :],
                                         op0=ALU.mult, op1=ALU.mult).then_inc(f_nb, 1)

            def f_scale(i, q, t):
                root = float(D) ** -0.5
                dve.wait_ge(f_had, i * 2 + t + 1)
                c = slice(t, t + 1)
                k = i * 10 + t * 5
                dve.tensor_reduce(amax[:, c], bank[7][:, :], AX.X, ALU.max,
                                  apply_absolute_value=True).then_inc(f_stat, 1)
                dve.wait_ge(f_stat, k + 1)
                dve.tensor_scalar(m1[:, c], amax[:, c], root, EPS, ALU.mult, ALU.max).then_inc(f_stat, 1)
                dve.wait_ge(f_stat, k + 2)
                dve.reciprocal(r1[:, c], m1[:, c]).then_inc(f_stat, 1)
                dve.wait_ge(f_stat, k + 3)
                dve.tensor_scalar(qs1[:, c], r1[:, c], 127.0 * root, None, ALU.mult).then_inc(f_qs, 1)
                dve.tensor_scalar(cg[:, c], m1[:, c], wscale[:, 0:1], 1.0 / 127, ALU.mult, ALU.mult).then_inc(f_stat, 1)
                dve.tensor_scalar(ku[q][:, c], m1[:, c], wscale[:, 1:2], float(FF) ** -0.5 / 127,
                                  ALU.mult, ALU.mult).then_inc(f_stat, 1)
                dve.wait_ge(f_stat, k + 5)
                dve.tensor_scalar(diag[:, t, :], ident[:, :], cg[:, c], None, ALU.mult).then_inc(f_diag, 1)

            def f_int(i, t):
                dve.wait_ge(f_qm, i * 2 + t + 1)
                dve.tensor_scalar(q_i[:, :], qm[:, :], -ROUND, 127.0, ALU.add, ALU.min).then_inc(f_qi, 1)

            def gate_scale(i, p, c):
                dve.wait_ge(gu_done, i * NP + c + 1)
                if c == 0:
                    dve.wait_ge(f_bro, i + 1)
                dve.tensor_tensor(z_sb[c % 2], bank[2 * (c % 2)][:, :], bro[p], ALU.mult).then_inc(z_ready, 1)

            def times_up(i, p, c):
                dve.wait_ge(s_ready, i * NP + c + 1)
                if c == 0 and exists(i - 2):
                    dve.wait_ge(y_done, i * 8 - 8)
                dve.tensor_tensor(h_a[p][:, 2 * c:2 * c + 2, :].rearrange("p c s -> p (c s)"),
                                  s_sb[c % 2], bank[2 * (c % 2) + 1][:, :], ALU.mult).then_inc(h_ready, 1)

            def stage_1(i, p, g):
                a = h_a[p][:, 4 * g:4 * g + 4, :].rearrange("p (u v) s -> p u v s", v=2)
                b_ = h_b[p][:, 4 * g:4 * g + 4, :].rearrange("p (u v) s -> p u v s", v=2)
                dve.wait_ge(h_ready, i * NP + 2 * g + 2)
                if g == 0 and exists(i - 2):
                    dve.wait_ge(b4_done, i * 4 - 4)
                dve.tensor_tensor(b_[:, :, 0, :], a[:, :, 0, :], a[:, :, 1, :], ALU.add).then_inc(b1_done, 1)
                dve.tensor_tensor(b_[:, :, 1, :], a[:, :, 0, :], a[:, :, 1, :], ALU.subtract).then_inc(b1_done, 1)

            def y_scale(i, q, t):
                p = q % 2
                c = slice(t, t + 1)
                k = i * 6 + t * 3
                dve.wait_ge(y_out_sem, i * 8 + 4 * t + 4)
                dve.tensor_reduce(amax2[:, c], y_sb[t], AX.X, ALU.max, apply_absolute_value=True).then_inc(y_stat, 1)
                dve.wait_ge(y_stat, k + 1)
                dve.tensor_scalar(m2[:, c], amax2[:, c], ku[q][:, c], EPS, ALU.mult, ALU.max).then_inc(y_stat, 1)
                dve.wait_ge(y_stat, k + 2)
                dve.reciprocal(r2[:, c], m2[:, c]).then_inc(y_stat, 1)
                dve.wait_ge(y_stat, k + 3)
                dve.tensor_scalar(qs2[:, c], r2[:, c], ku[q][:, c], 127.0, ALU.mult, ALU.mult).then_inc(y_qs, 1)
                dve.tensor_scalar(dd[p][:, c], m2[:, c], wscale[:, 2:3], 1.0 / 127, ALU.mult, ALU.mult).then_inc(dd_ready, 1)

            def y_int(i, t):
                dve.wait_ge(y_qm, i * 2 + t + 1)
                if exists(i - 1):
                    dve.wait_ge(q2_turned, i * 4 - 2 + 2 * t)
                dve.tensor_scalar(q2_i[:, t, :], y_sb[t], -ROUND, 127.0, ALU.add, ALU.min).then_inc(y_qi, 1)

            def finish(i, p, t):
                dve.wait_ge(d_done, i * 2 + t + 1)
                if exists(i - 1):
                    dve.wait_ge(stored[t], i * 16)
                if t == 0:
                    dve.wait_ge(r_loaded[p], (i // 2) * 16 + 16 if isinstance(i, int) else (i - p) * 8 + 16)
                    dve.wait_ge(dd_ready, i * 2 + 2)
                dve.scalar_tensor_tensor(out=y_out[t][:, :], in0=bank[6][:, :], scalar=dd[p][:, t:t + 1],
                                         in1=x_res[p][:, t, :], op0=ALU.mult, op1=ALU.add).then_inc(o2_ready, 1)

            f_norm(0, 0)
            f_shift(0)
            for t in range(TT):
                f_scale(0, 0, t)
                f_int(0, t)
            f_norm(1, 1)
            f_shift(1)

            def body2(i, q):
                p = q % 2
                here, before, two, ahead = exists(i, B), exists(i - 1, B), exists(i - 2, B), exists(i + 1, B)
                for c in range(NP):
                    if here:
                        gate_scale(i, p, c)
                    if c == 0 and two:
                        y_int(i - 2, 0)
                    if c == 1 and ahead:
                        f_scale(i + 1, (q + 1) % 4, 0)
                    if c == 2 and ahead:
                        f_int(i + 1, 0)
                    if c == 2 and two:
                        y_int(i - 2, 1)
                    if c == 3 and two:
                        finish(i - 2, p, 0)
                    if c == 4 and exists(i + 2, B):
                        f_norm(i + 2, p)
                    if c == 5 and exists(i + 2, B):
                        f_shift(i + 2)
                    if c == 5 and ahead:
                        f_scale(i + 1, (q + 1) % 4, 1)
                    if c == 6 and ahead:
                        f_int(i + 1, 1)
                    if here:
                        times_up(i, p, c)
                        if c % 2 == 1:
                            stage_1(i, p, c // 2)
                    if c == 0 and two:
                        y_scale(i - 2, (q + 2) % 4, 1)
                    if c == 5 and two:
                        finish(i - 2, p, 1)
                    if c == 6 and before:
                        y_scale(i - 1, (q + 3) % 4, 0)

            quads(dve, body2, B)
            body2(B, 0)
            body2(B + 1, 1)

        @block.tensor
        def _(pe):
            pe.wait_ge(const_ok, 5)
            for m in range(3):
                pe.wait_ge(w_summed, m + 1)
                pe.matmul(bank[4][:, m:m + 1], ones[:, :], wcol[:, m:m + 1], start=True, stop=True).then_inc(w_total, 1)
                pe.wait_ge(w_tern, m + 1)
                for n in range(m * WT // 2, (m + 1) * WT // 2):
                    if n >= 4:
                        pe.wait_ge(w_out_a if n % 2 else w_out_d, (n - 4) // 2 + 1)
                    for k in range(8):
                        t = 2 * n - m * WT + k // 4
                        ins = pe.transpose(bank[n % 4][:, 64 * k:64 * k + 64].bitcast(BF16),
                                           tern[:, t, (k % 4) * P:(k % 4 + 1) * P], identb[:, :])
                    ins.then_inc(w_turned, 1)
            pe.wait_ge(w_out_a, 3 * WT // 4)
            pe.wait_ge(w_out_d, 3 * WT // 4)
            pe.wait_ge(w_turned, 3 * WT // 2)

            def turn(b, p, k):
                t = k // 2
                if k == 0:
                    pe.wait_ge(xn_ready, b * 2 + 2)
                    pe.wait_ge(c_loaded[p], (b // 2) * 16 + 16 if isinstance(b, int) else (b - p) * 8 + 16)
                if not (isinstance(b, int) and b == 0 and k == 0):
                    pe.wait_ge(turned_a, b * 4 + k)
                    if k % 2 == 0:
                        pe.wait_ge(turned_d, b * 2 + k // 2)
                src = (c_in if k % 2 else xn)[p]
                for g in range(GROUPS):
                    ins = pe.transpose(bank[X_BANK][:, g * P:(g + 1) * P], src[:, t, g * P:(g + 1) * P], ident[:, :])
                ins.then_inc(turned, 1)

            def score(b, p, s):
                t, g, h0, heads, keys = step_of(s)
                if s in (0, 4):
                    pe.wait_ge(turned_a, b * 4 + 2 * t + 2)
                    pe.wait_ge(turned_d, b * 2 + t + 1)
                if not (isinstance(b, int) and b * STEPS + s < 3):
                    pe.wait_ge(exp_done, b * STEPS + s - 2)
                o = bank[S_BANK[s % 3]]
                pe.matmul(o[:, :].rearrange("p (h k) -> p h k", h=heads), q_t[p][:, g, t * P:(t + 1) * P],
                          k_z[p][:, g, h0:h0 + heads, 0:keys], start=True, stop=False)
                pe.matmul(o[:, :].rearrange("p (h k) -> p h k", h=heads)[:, :, keys - P:keys], identb[:, :],
                          maskb[:, 0:heads, :], start=False, stop=True).then_inc(scored, 1)

            def turn_p(b, s):
                n = b * STEPS + s
                pe.wait_ge(exp_done, n + 1)
                if not (isinstance(b, int) and b * STEPS + s < 2):
                    if s % 2:
                        pe.wait_ge(pt_dve, b * 6 + s // 2)
                    else:
                        pe.wait_ge(pt_act, b * 6 + s // 2)
                for k in range(4):
                    ins = pe.transpose(bank[T_BANK[s % 2]][:, k * P:(k + 1) * P],
                                       prob[s % 3][:, k * P:(k + 1) * P], ident[:, :])
                ins.then_inc(p_turned, 1)

            def pv(b, p, s):
                t, g, h0, heads, keys = step_of(s)
                u = unit_of(s)
                if s in (0, 2, 4, 8) and not (isinstance(b, int) and b == 0 and s < 4):
                    pe.wait_ge(o_ready, b * 4 + u - 1)
                if s == 0:
                    pe.wait_ge(v_ready, b + 1)
                if s % 2:
                    pe.wait_ge(pt_dve, b * 6 + s // 2 + 1)
                else:
                    pe.wait_ge(pt_act, b * 6 + s // 2 + 1)
                kb = keys // P
                for h in range(heads):
                    head = 4 * g + h0 + h
                    e = (head % 8) * (HD + 1)
                    for k in range(kb):
                        c = (h * kb + k) * P
                        ins = pe.matmul(bank[O_BANK[u % 2]][:, e:e + HD + 1], prob_t[s % 3][:, c:c + P],
                                        v_a[p][:, k, head, :], start=(k == 0), stop=(k == kb - 1))
                ins.then_inc(pv_done, 1)

            for k in range(3):
                turn(0, 0, k)

            def body(b, odd=0):
                p = par(b, odd)
                more = not (isinstance(b, int) and b + 1 >= B)
                for s in range(STEPS):
                    score(b, p, s)
                    if s >= LAG_T:
                        turn_p(b, s - LAG_T)
                    elif exists(b - 1):
                        turn_p(b - 1, s - LAG_T + STEPS)
                    if s >= LAG_V:
                        pv(b, p, s - LAG_V)
                    elif exists(b - 1):
                        pv(b - 1, 1 - p, s - LAG_V + STEPS)
                    for k in range(4):
                        if s == TURN[k] and more:
                            turn(b + 1, 1 - p, k)
                        if s == TURN[k] - STEPS:
                            turn(b, p, k)

            batches(pe, body, B)
            turn_p(B - 1, STEPS - 2)
            pv(B - 1, 1, STEPS - 3)
            turn_p(B - 1, STEPS - 1)
            pv(B - 1, 1, STEPS - 2)
            pv(B - 1, 1, STEPS - 1)

            pe.wait_ge(o_ready, B * 4)

            def prep_turn(i, t):
                if t == 0:
                    pe.wait_ge(f_rot, i * 8 + 8)
                if exists(i - 1) or t:
                    pe.wait_ge(f_xq, i * 2 + t)
                for c in range(KC):
                    ins = pe.transpose(bank[7][:, c * P:(c + 1) * P], r_a[:, t, c, :], ident[:, :])
                ins.then_inc(f_rot_t, 1)

            def prep_had(i, t):
                pe.wait_ge(f_rot_e, i * 2 + t + 1)
                for c in range(KC):
                    ins = pe.matmul(bank[7][:, c * P:(c + 1) * P], rot_t[:, c, :], had[:, :], start=True, stop=True)
                ins.then_inc(f_had, 1)

            def prep_int(i, t):
                pe.wait_ge(f_qi, i * 2 + t + 1)
                if t == 1:
                    pe.wait_ge(f_bro, i + 1)
                for c in range(KC):
                    ins = pe.transpose(bank[7][:, 64 * c:64 * c + 64].bitcast(BF16),
                                       q_i[:, c * P:(c + 1) * P], identb[:, :])
                ins.then_inc(f_qt, 1)

            def prep_scales(i):
                pe.wait_ge(f_qi, i * 2 + 2)
                pe.wait_ge(f_diag, i * 2 + 2)
                for k in range(2):
                    ins = pe.matmul(bank[7][:, k * S:(k + 1) * S], ones[:, :],
                                    diag[:, :, :].rearrange("p t f -> p (t f)"), start=True, stop=True)
                ins.then_inc(f_brop, 1)

            def gate_up(i, p, c):
                if c == 0:
                    pe.wait_ge(f_xq, i * 2 + 2)
                if not (isinstance(i, int) and i * NP + c < 2):
                    pe.wait_ge(h_ready, i * NP + c - 1)
                for w, o in ((gate_t, bank[2 * (c % 2)]), (up_t, bank[2 * (c % 2) + 1])):
                    for h in range(2):
                        for k in range(KC):
                            f = (2 * c + h) * P
                            ins = pe.matmul(o[:, h * S:(h + 1) * S], w[:, k, f:f + P], xq_t[p][:, k, :],
                                            start=(k == 0), stop=(k == KC - 1))
                ins.then_inc(gu_done, 1)

            def transform(i, p, t, q):
                if q == 0:
                    pe.wait_ge(b4_done, i * 4 + 2 * t + 2)
                if t == 0 and q < 2:
                    if exists(i - 1):
                        pe.wait_ge(q2_ready, i * 4 - 1 + q)
                else:
                    pe.wait_ge(y_out_sem, i * 8 + 4 * t + q - 1)
                for k in range(4):
                    ins = pe.matmul(bank[4 + q % 2][:, k * P:(k + 1) * P], h_a[p][:, 4 * q + k, t * P:(t + 1) * P],
                                    had[:, :], start=True, stop=True)
                ins.then_inc(y_done, 1)

            def turn_q2(i, t, k):
                if k == 0:
                    pe.wait_ge(y_qi, i * 2 + t + 1)
                if t == 0:
                    pe.wait_ge(y_out_sem, i * 8 + 7 + k)
                else:
                    pe.wait_ge(q2_ready, i * 4 + 1 + k)
                for c in range(8):
                    ins = pe.transpose(bank[4 + k][:, 64 * c:64 * c + 64].bitcast(BF16),
                                       q2_i[:, t, (8 * k + c) * P:(8 * k + c + 1) * P], identb[:, :])
                ins.then_inc(q2_turned, 1)

            def down(i, t):
                pe.wait_ge(q2_ready, i * 4 + 2 * t + 2)
                if not (isinstance(i, int) and i == 0 and t == 0):
                    pe.wait_ge(o2_ready, i * 2 + t)
                for c in range(NC):
                    ins = pe.matmul(bank[6][:, :], q2_t[:, t, c, :], down_t[:, c, :],
                                    start=(c == 0), stop=(c == NC - 1))
                ins.then_inc(d_done, 1)

            for t in range(TT):
                prep_turn(0, t)
                prep_had(0, t)
                if t == 1:
                    prep_scales(0)
                prep_int(0, t)

            def body2(i, odd=0):
                p = par(i, odd)
                here, before, two, ahead = exists(i, B), exists(i - 1, B), exists(i - 2, B), exists(i + 1, B)
                for c in range(NP):
                    if here:
                        gate_up(i, p, c)
                    if c == 0 and ahead:
                        prep_turn(i + 1, 0)
                    if c == 1 and ahead:
                        prep_had(i + 1, 0)
                    if c == 1 and two:
                        turn_q2(i - 2, 0, 0)
                        turn_q2(i - 2, 0, 1)
                    if c == 2 and two:
                        down(i - 2, 0)
                    if c == 3 and ahead:
                        prep_int(i + 1, 0)
                    if c == 3 and two:
                        turn_q2(i - 2, 1, 0)
                        turn_q2(i - 2, 1, 1)
                    if c == 4 and ahead:
                        prep_turn(i + 1, 1)
                    if c == 4 and two:
                        down(i - 2, 1)
                    if c == 5 and ahead:
                        prep_had(i + 1, 1)
                    if c == 7 and ahead:
                        prep_scales(i + 1)
                    if c >= 4 and before:
                        for q in (2 * (c - 4), 2 * (c - 4) + 1):
                            transform(i - 1, 1 - p, q // 4, q % 4)
                    if c == 7 and ahead:
                        prep_int(i + 1, 1)

            batches(pe, body2, B)
            body2(B)
            body2(B + 1)


def kernel(**inputs):
    import concourse.bacc as bacc
    from concourse.bass_utils import run_bass_kernel_spmd

    bits = np.array([[bin(a & b).count("1") for b in range(P)] for a in range(P)])
    arrays = {name: np.ascontiguousarray(inputs[name]) for name in
              ("x", "ctx_2048", "L0_ffn_w_gate", "L0_ffn_w_up", "L0_ffn_w_down")}
    arrays["identity"] = np.eye(P, dtype=np.float32)
    arrays["hadamard"] = (1 - 2 * (bits % 2)).astype(np.float32)
    arrays["causal"] = np.triu(np.full((P, P), MASKED, np.float32), 1)
    nc = bacc.Bacc("TRN2", target_bir_lowering=False, num_devices=1)
    args = [nc.dram_tensor(name, a.shape, mybir.dt.from_np(a.dtype), kind="ExternalInput").ap()
            for name, a in arrays.items()]
    shape = arrays["x"].shape
    args.append(nc.dram_tensor("out", shape, F32, kind="ExternalOutput").ap())
    attention_ffn(nc, *args)
    result = run_bass_kernel_spmd(nc, [arrays], core_ids=[0])
    return result.results[0]["out"]
```
